# Optimizing a Trainium2 kernel written in Bass

```python
import numpy as np
import jax
import jax.numpy as jnp

def _softmax(x, axis=-1):
    return jax.nn.softmax(x, axis=axis)

def _gelu(x):
    return jax.nn.gelu(x, approximate=True)

def _silu(x):
    return jax.nn.silu(x)

def _sigmoid(x):
    return jax.nn.sigmoid(x)

def _layernorm(x, axis=-1, eps=1e-05):
    m = jnp.mean(x, axis=axis, keepdims=True)
    v = jnp.var(x, axis=axis, keepdims=True)
    return (x - m) / jnp.sqrt(v + eps)

def _scatter_add(tgt, idx, src, axis=0):
    return tgt.at[idx].add(src)

def _segment_sum(src, seg, n):
    return jax.ops.segment_sum(src, seg, n)
kernel_name = 'mk_gnn_resnorm_d1_gnn_r32_89f8e5'

def setup_inputs(seed: int=0):
    np.random.seed(seed)
    _w = jnp.asarray

    def _rec_inputs():
        import jax
        import jax.numpy as jnp
        _gk = jax.random.key(seed)
        x = -0.0002117 + 1 * jax.random.normal(jax.random.fold_in(_gk, 1), (10000, 512), jnp.float32)
        src = jax.random.randint(jax.random.fold_in(_gk, 2), (10000,), 0, 10000, jnp.int32)
        dst = jnp.minimum((10000 * jax.random.uniform(jax.random.fold_in(_gk, 3), (10000,)) ** 2.0).astype(jnp.int32), 9999)
        _o = jnp.argsort(dst, stable=True)
        src = src[_o]
        dst = dst[_o]
        return (x, src, dst)
    x, src, dst = _rec_inputs()

    def _L0_gnn_setup():
        import jax, jax.numpy as jnp
        import numpy as np
        from functools import partial
        N_NODES = 50000
        N_EDGES = 5000
        D = 512
        N_LAYERS = 8
        LN_EPS = 1e-05

        def _layer_norm(x, g, b):
            mu = jnp.mean(x, axis=-1, keepdims=True)
            var = jnp.mean(jnp.square(x - mu), axis=-1, keepdims=True)
            return (x - mu) * jax.lax.rsqrt(var + LN_EPS) * g + b
        key = jax.random.key(seed)
        ks = jax.random.split(key, 4)
        features = jax.random.normal(ks[0], (N_NODES, D), dtype=jnp.float32)
        src = jax.random.randint(ks[1], (N_EDGES,), 0, N_NODES, dtype=jnp.int64)
        dst = jax.random.randint(ks[2], (N_EDGES,), 0, N_NODES, dtype=jnp.int64)
        Ws = jax.random.normal(ks[3], (N_LAYERS, D, D), dtype=jnp.float32) * (1.0 / np.sqrt(D))
        bs = jnp.zeros((N_LAYERS, D), dtype=jnp.float32)
        ln_g = jnp.ones((N_LAYERS, D), dtype=jnp.float32)
        ln_b = jnp.zeros((N_LAYERS, D), dtype=jnp.float32)
        return {'features': features, 'src': src, 'dst': dst, 'Ws': Ws, 'bs': bs, 'ln_g': ln_g, 'ln_b': ln_b}
    _L0_gnn_all = _L0_gnn_setup()
    _L0_gnn_in = {k: v for k, v in _L0_gnn_all.items() if k in ('Ws', 'bs', 'ln_g', 'ln_b')}
    del _L0_gnn_all
    return {'x': x, 'src': src, 'dst': dst, 'L0_gnn_Ws': _L0_gnn_in['Ws'], 'L0_gnn_bs': _L0_gnn_in['bs'], 'L0_gnn_ln_g': _L0_gnn_in['ln_g'], 'L0_gnn_ln_b': _L0_gnn_in['ln_b']}

def reference(x, src, dst, L0_gnn_Ws, L0_gnn_bs, L0_gnn_ln_g, L0_gnn_ln_b):
    import jax
    import jax.numpy as jnp

    def _L0_gnn_ref(features, src, dst, Ws, bs, ln_g, ln_b):
        import jax, jax.numpy as jnp
        import numpy as np
        from functools import partial
        N_NODES = 50000
        N_EDGES = 5000
        D = 512
        N_LAYERS = 8
        LN_EPS = 1e-05

        def _layer_norm(x, g, b):
            mu = jnp.mean(x, axis=-1, keepdims=True)
            var = jnp.mean(jnp.square(x - mu), axis=-1, keepdims=True)
            return (x - mu) * jax.lax.rsqrt(var + LN_EPS) * g + b
        n = features.shape[0]
        ones_e = jnp.ones(src.shape[0], dtype=features.dtype)
        deg_out = jnp.clip(jax.ops.segment_sum(ones_e, src, num_segments=n), 1.0)
        deg_in = jnp.clip(jax.ops.segment_sum(ones_e, dst, num_segments=n), 1.0)
        norm_out = jax.lax.rsqrt(deg_out)[:, None]
        norm_in = jax.lax.rsqrt(deg_in)[:, None]

        def layer(h, params):
            W, b, g, beta = params
            h = h * norm_out
            agg = jax.ops.segment_sum(h[src], dst, num_segments=n)
            agg = agg * norm_in
            out = agg @ W + b
            out = _layer_norm(out, g, beta)
            out = jax.nn.gelu(out, approximate=False)
            return (out, None)
        h, _ = jax.lax.scan(layer, features, (Ws, bs, ln_g, ln_b))
        return h
    x = _layernorm(x + _L0_gnn_ref(x, src, dst, L0_gnn_Ws, L0_gnn_bs, L0_gnn_ln_g, L0_gnn_ln_b), axis=-1)
    return x

_drawn_inputs = setup_inputs


def setup_inputs(seed=0):
    import zlib

    import numpy as np

    out = dict(_drawn_inputs(seed))
    spreads = {'L0_gnn_bs': (0.0, 0.1), 'L0_gnn_ln_g': (1.0, 0.2), 'L0_gnn_ln_b': (0.0, 0.1)}
    factors = {}
    for name, (base, spread) in spreads.items():
        noise = np.random.default_rng([zlib.crc32(name.encode()), seed]).standard_normal(out[name].shape)
        drawn = base * np.exp(spread * noise) if base else spread * noise
        out[name] = jnp.asarray(drawn.astype(out[name].dtype))
    for name, factor in factors.items():
        out[name] = (out[name] * factor).astype(out[name].dtype)
    return out
```

```python
import concourse.bass as bass
from concourse import mybir
from contextlib import ExitStack

N = 10000
E = 10000
D = 512
LAYERS = 8
EPS = 1e-5
P = 128
KB = D // P
ET = P - 1
NE = 80
NR = 80
PADDED = NR * P
GS = 4
COLS = 8
C_LAST, C_MID, C_NIN, C_NINM, C_NOUT, C_ROW = range(6)
PRIME = 8

f32, f32r, i32, bf16 = mybir.dt.float32, mybir.dt.float32r, mybir.dt.int32, mybir.dt.bfloat16
ALU = mybir.AluOpType
ACT = mybir.ActivationFunctionType


def done(n):
    return n + PRIME


def build(nc, x, src, dst, Ws, bs, ln_g, ln_b, out):
    hbuf = nc.dram_tensor("h_rows", (PADDED, D), f32).ap()
    ntab_d = nc.dram_tensor("node_table", (PADDED, COLS), f32).ap()
    ctx = ExitStack()
    with ctx:
        def sb(n, s, d=f32):
            return ctx.enter_context(nc.sbuf_tensor(n, s, d))

        def sem(n):
            return ctx.enter_context(nc.semaphore(n))

        agg_t = sb("agg_t", [P, KB, PADDED])
        w_hi = sb("w_hi", [P, KB, D], f32r)
        w_lo = sb("w_lo", [P, KB, D], f32r)
        w_raw = sb("w_raw", [P, 2, D])
        b_rows = sb("b_rows", [2, D], f32r)
        zcol = sb("zcol", [P, KB])
        b_raw = w_raw
        gam = sb("gam", [P, D])
        bet = sb("bet", [P, D])
        s_hi = sb("s_hi", [P, 2, KB, P], f32r)
        s_lo = sb("s_lo", [P, 2, KB, P], f32r)
        b_high = s_hi[0:2, 0, :, :].rearrange("p a b -> p (a b)")
        rows = sb("rows", [P, GS, D])
        sel = sb("sel", [P, 2, P])
        iota = sb("iota", [P, P])
        ones2 = sb("ones2", [2, P], f32r)
        negm = sb("negm", [2, 1])
        idx_x = sb("idx_x", [P, NE], i32)
        idx_h = sb("idx_h", [P, NE], i32)
        idx_f = sb("idx_f", [P, NR], i32)
        wgt_m = sb("wgt_m", [P, NE + 2])
        wgt_l = sb("wgt_l", [P, NE + 2])
        rel_m = sb("rel_m", [P, NE + 2])
        rel_l = sb("rel_l", [P, NE + 2])
        q0_m = sb("q0_m", [1, NE], i32)
        q0_l = sb("q0_l", [1, NE], i32)
        counts = sb("counts", [1, 2], i32)
        slot = sb("slot", [P, GS], i32)
        slot2 = sb("slot2", [P, GS], i32)
        stats = sb("stats", [P, GS, 6])
        mv = sb("mv", [P, GS, 2])
        var = sb("var", [P, GS])
        rstd = sb("rstd", [P, GS])
        mhalf = sb("mhalf", [P, 1])

        ps_a = [ctx.enter_context(nc.psum_tensor(f"ps_a{i}", [P, KB, P], f32)) for i in range(2)]
        ps_y = [ctx.enter_context(nc.psum_tensor(f"ps_y{i}", [P, D], f32)) for i in range(2)]
        ps_s = [ctx.enter_context(nc.psum_tensor(f"ps_s{i}", [P, D], f32)) for i in range(2)]

        class Space:
            at = 0

        def part(shape, d=f32):
            size = 1
            for v in shape[1:]:
                size *= v
            words = size * (2 if d is bf16 else 4) // 4
            flat = agg_t[:, :, :].rearrange("p k n -> p (k n)")[0:shape[0], Space.at:Space.at + words]
            Space.at += words
            if d is not f32:
                flat = flat.bitcast(d)
            if len(shape) == 3:
                flat = flat.rearrange("p (a b) -> p a b", b=shape[2])
            return flat

        src_i = part([P, NE], i32)
        dst_i = part([P, NE], i32)
        hilo_i = part([P, 4, NE], i32)
        hilo = part([P, 4, NE])
        hot = [part([P, NE, n], bf16) for n in (NR, P, NR, P)]
        zero_bf = part([P, P], bf16)
        zero_row = part([P, D])
        node_i = part([NR, P], i32)
        iota_i = part([P, P], i32)
        valid = part([NR, P])
        outs, ins = part([NR, P]), part([NR, P])
        act_l, act_m = part([NR, P]), part([NR, P])
        row_sums = part([NR, 2])
        scan_l, scan_m = part([NR, P]), part([NR, P])
        before = part([NR, 2])
        totals = part([P, 2])
        ones_np = part([NR, P])
        lower = part([NR, NR])
        power = part([NR, P])
        ntab = part([NR, P, COLS])
        t1, t2, t3 = part([NR, P]), part([NR, P]), part([NR, P])
        fidx = part([NR, P])
        ident = part([P, P])
        pick = part([P, P])
        dtab = part([P, NE, COLS])
        stab = part([P, NE, COLS])
        dslot = part([P, GS, COLS])
        sslot = part([P, GS, COLS])
        q0b = part([P, 2, NE])
        cnt_f, cnt_i, cnt_i2 = part([1, 2]), part([1, 2], i32), part([1, 2], i32)
        Space.at = 0
        xs = part([P, GS, D])
        hf = part([P, GS, D])
        of = part([P, GS, D])

        hot_ok = sem("one_hots_made")
        hist_ok = sem("histograms_done")
        deg_ok = sem("degrees_clipped")
        pow_ok = sem("norms_made")
        sums_ok = sem("row_sums_made")
        pre_ok = sem("prefix_done")
        fid_ok = sem("final_index_made")
        fidt_ok = sem("final_index_transposed")
        table_ok = sem("node_table_made")
        kept_ok = sem("all_table_rows_kept")
        pick_ok = sem("first_ranks_spread")
        v_step = sem("vector_steps")
        p_step = sem("pool_setup_steps")
        rows_clear = sem("zero_row_made")
        h_clear = sem("h_cleared")
        nt_st = sem("node_table_stored")
        tick = sem("pool_ticks")
        cp_idx = sem("index_copied")
        tg_d = [sem(f"dst_row_in{k}") for k in range(GS)]
        tg_s = [sem(f"src_row_in{k}") for k in range(GS)]
        tg_cp = sem("table_rows_kept")
        setup_ok = sem("setup_done")
        g_in = [sem(f"rows_gathered{k}") for k in range(GS)]
        sel_ok = sem("selection_made")
        agg_ok = sem("tile_summed")
        ev_ok = sem("sums_kept")
        edge_ok = sem("first_column_added")
        raw_in = [sem(f"w_chunk_in{k}") for k in range(2)]
        b_in = sem("bias_in")
        gb_in = sem("gamma_beta_in")
        w_ok = sem("w_chunk_split")
        b_ok = sem("bias_split")
        hi_ok = sem("high_half_made")
        lo_ok = sem("low_half_made")
        y_ok = sem("product_done")
        st_ok = sem("stats_made")
        act_tick = sem("act_ticks")
        dve_tick = sem("dve_ticks")
        mv_ok = sem("mean_var_made")
        var_ok = sem("var_eps_made")
        rs_ok = sem("rstd_made")
        t_ok = sem("centred")
        u_ok = sem("normalised")
        h_ok = sem("gelu_done")
        h_st = [sem(f"h_stored{k}") for k in range(2)]
        pe_tick = sem("pe_ticks")
        sp_tick = sem("sp_ticks")
        wh_ok = sem("w_high_made")
        bh_ok = sem("bias_high_made")
        v_tail = sem("tail_cleared")
        zero_ok = sem("column_cleared")
        xf_in = [sem(f"x_tile_in{k}") for k in range(GS)]
        hf_in = [sem(f"h_tile_in{k}") for k in range(GS)]
        f_sum = sem("residual_added")
        f_st = sem("final_stats")
        f_mv = sem("final_mean_var")
        f_ve = sem("final_var_eps")
        f_rs = sem("final_rstd")
        f_o = sem("final_rows_made")
        o_st = [sem(f"out_stored{k}") for k in range(GS)]
        o_last = sem("out_tail_stored")

        block = ctx.enter_context(nc.Block())
        EDGE_TILES_PER_CHUNK = NE // KB

        def tile_counts(eng):
            eng.wait_ge(setup_ok, 1)
            mid = eng.value_load(counts[0:1, 0:1], min_val=2, max_val=NR // 2)
            last = eng.value_load(counts[0:1, 1:2], min_val=2, max_val=NR // 2)
            return mid, last, mid * 2, last * 2

        FULL = N // P
        TAIL = N - FULL * P
        FLOOP = FULL // GS * GS

        def final_tiles(eng, tile):
            with eng.Fori(0, FLOOP // GS) as group:
                t = group * GS
                for k in range(GS):
                    tile(t, k, P)
            for k in range(FULL - FLOOP):
                tile(FLOOP, k, P)
            tile(FLOOP, FULL - FLOOP, TAIL)

        @block.sync
        def _(sp):
            sp.dma_start(src_i, src).then_inc(h_st[0], 16)
            sp.dma_start(dst_i, dst).then_inc(h_st[1], 16)
            sp.wait_ge(rows_clear, 1)
            sp.dma_start(hbuf.rearrange("(a p) n -> p a n", p=P),
                         zero_row.unsqueeze(1).to_broadcast([P, NR, D])).then_inc(h_clear, 16)
            sp.wait_ge(table_ok, 1)
            sp.dma_start(ntab_d.rearrange("(a b) c -> a b c", b=P), ntab).then_inc(nt_st, 16)
            sp.wait_ge(h_clear, 16)
            pairs_m, pairs_l, nbm, nbl = tile_counts(sp)

            def layer(L, pairs):
                base = L * nbm
                for q in range(KB):
                    sp.wait_ge(w_ok, done(L * KB + q - 1))
                    sp.sem_inc(sp_tick, 1)
                    if q == 0:
                        sp.wait_ge(b_ok, done(L))
                        sp.sem_inc(sp_tick, 1)
                    sp.dma_start(w_raw[:, q % 2, :], Ws[bass.ds(L, 1), q * P:(q + 1) * P, :]
                                 .rearrange("a p n -> p (a n)")).then_inc(raw_in[q % 2], 16)
                sp.wait_ge(u_ok, done(base))
                sp.sem_inc(sp_tick, 1)
                sp.dma_start(gam[:, :], ln_g[bass.ds(L, 1), :].rearrange("a n -> (a n)")
                             .partition_broadcast(P)).then_inc(gb_in, 16)
                sp.dma_start(bet[:, :], ln_b[bass.ds(L, 1), :].rearrange("a n -> (a n)")
                             .partition_broadcast(P)).then_inc(gb_in, 16)
                sp.wait_ge(w_ok, done(L * KB + KB))
                sp.sem_inc(sp_tick, 1)
                sp.dma_start(b_raw[0:2, 0, :], bs[bass.ds(L, 1), :].rearrange("a n -> (a n)")
                             .partition_broadcast(2)).then_inc(b_in, 16)
                with sp.Fori(0, pairs) as pair:
                    c = pair * 2
                    for k in range(2):
                        j = base + c
                        sp.wait_ge(h_ok, done(j + k + 1))
                        sp.sem_inc(sp_tick, 1)
                        sp.dma_start(hbuf[bass.ds((c + k) * P, P), :], rows[:, 2 + k, :])\
                          .then_inc(h_st[k], 16)

            with sp.Fori(0, LAYERS - 1) as L:
                layer(L, pairs_m)
            layer(LAYERS - 1, pairs_l)
            sp.wait_ge(lo_ok, done((LAYERS - 1) * nbm + nbl))
            sp.sem_inc(sp_tick, 1)

            def load(t, k, n):
                if not isinstance(t, int):
                    sp.wait_ge(f_o, done(t + k - GS + 1))
                    sp.sem_inc(sp_tick, 1)
                sp.dma_start(xs[0:n, k, :], x[bass.ds((t + k) * P, n), :]).then_inc(xf_in[k], 16)

            def store(t, k, n):
                sp.wait_ge(f_o, done(t + k + 1))
                sp.sem_inc(sp_tick, 1)
                sp.dma_start(out[bass.ds((t + k) * P, n), :], of[0:n, k, :])\
                  .then_inc(o_st[k] if n == P else o_last, 16)

            for k in range(GS):
                load(0, k, P)
            with sp.Fori(0, (FLOOP - GS) // GS) as group:
                t = group * GS
                for k in range(GS):
                    store(t, k, P)
                    load(t + GS, k, P)
            for k in range(GS):
                store(FLOOP - GS, k, P)
                if FLOOP + k < FULL:
                    sp.dma_start(xs[:, k, :], x[(FLOOP + k) * P:(FLOOP + k + 1) * P, :]).then_inc(xf_in[k], 16)
                elif FLOOP + k == FULL:
                    sp.dma_start(xs[0:TAIL, k, :], x[FULL * P:N, :]).then_inc(xf_in[k], 16)
            for k in range(FULL - FLOOP):
                store(FLOOP, k, P)
            store(FLOOP, FULL - FLOOP, TAIL)
            for k in range(GS):
                sp.wait_ge(o_st[k], 16 * (FLOOP // GS + (FLOOP + k < FULL)))
            sp.wait_ge(o_last, 16)

        @block.gpsimd
        def _(pool):
            g = nc.gpsimd
            for s in (rs_ok, var_ok, cp_idx):
                pool.sem_inc(s, PRIME)
            g.memset(zero_row, 0.0).then_inc(rows_clear, 1)
            g.iota(node_i, pattern=[[1, P]], base=0, channel_multiplier=P).then_inc(p_step, 1)
            g.iota(iota_i, pattern=[[1, P]], base=0, channel_multiplier=0).then_inc(p_step, 1)
            g.memset(mhalf[:, :], -0.5).then_inc(p_step, 1)
            g.memset(power, -0.5).then_inc(p_step, 1)
            g.memset(ones_np, 1.0).then_inc(p_step, 1)
            g.memset(lower, 1.0).then_inc(p_step, 1)
            g.memset(ident, 0.0).then_inc(p_step, 1)
            g.memset(pick, 1.0).then_inc(p_step, 1)
            g.memset(negm[:, :], -1.0).then_inc(p_step, 1)
            pool.wait_ge(p_step, 9)
            g.affine_select(out=lower, in_=lower, compare_op=ALU.is_gt, fill=0.0, base=0,
                            pattern=[[1, NR]], channel_multiplier=-1).then_inc(p_step, 1)
            g.affine_select(out=ident, in_=ident, compare_op=ALU.not_equal, fill=1.0, base=0,
                            pattern=[[-1, P]], channel_multiplier=1).then_inc(p_step, 1)
            g.affine_select(out=pick, in_=pick, compare_op=ALU.is_equal, fill=0.0, base=-(ET - 1),
                            pattern=[[0, P]], channel_multiplier=1).then_inc(p_step, 1)
            g.affine_select(out=negm[:, :], in_=negm[:, :], compare_op=ALU.not_equal, fill=0.0, base=0,
                            pattern=[[0, 1]], channel_multiplier=1).then_inc(p_step, 1)
            pool.wait_ge(deg_ok, 2)
            g.tensor_tensor(t1, t1, power, ALU.pow).then_inc(pow_ok, 1)
            g.tensor_tensor(t2, t2, power, ALU.pow).then_inc(pow_ok, 1)
            pool.wait_ge(nt_st, 16)
            with pool.Fori(0, NE // GS) as group:
                i = group * GS
                for k in range(GS):
                    pool.wait_ge(tg_cp, done(2 * (i + k - GS + 1)))
                    pool.sem_inc(tick, 1)
                    g.tensor_copy(slot[:, k:k + 1], dst_i[:, bass.ds(i + k, 1)]).then_inc(cp_idx, 1)
                    g.tensor_copy(slot2[:, k:k + 1], src_i[:, bass.ds(i + k, 1)]).then_inc(cp_idx, 1)
                    pool.wait_ge(cp_idx, done(2 * (i + k + 1)))
                    pool.sem_inc(tick, 1)
                    g.indirect_dma_start(out=dslot[:, k, :], out_offset=None, in_=ntab_d[:, :],
                                         in_offset=bass.IndirectOffsetOnAxis(ap=slot[:, k:k + 1], axis=0))\
                     .then_inc(tg_d[k], 16)
                    g.indirect_dma_start(out=sslot[:, k, :], out_offset=None, in_=ntab_d[:, :],
                                         in_offset=bass.IndirectOffsetOnAxis(ap=slot2[:, k:k + 1], axis=0))\
                     .then_inc(tg_s[k], 16)
            pairs_m, pairs_l, nbm, nbl = tile_counts(pool)
            IDX0 = 2 * NE

            def sum_stage(L, table, idx):
                with pool.Fori(0, NE // GS) as group:
                    t = group * GS
                    for k in range(GS):
                        i = L * NE + t
                        pool.wait_ge(agg_ok, done(i + k - GS + 1))
                        pool.sem_inc(tick, 1)
                        g.tensor_copy(slot[:, k:k + 1], idx[:, bass.ds(t + k, 1)]).then_inc(cp_idx, 1)
                        pool.wait_ge(cp_idx, done(IDX0 + i + k + 1))
                        pool.sem_inc(tick, 1)
                        g.indirect_dma_start(out=rows[:, k, :], out_offset=None, in_=table[:, :],
                                             in_offset=bass.IndirectOffsetOnAxis(ap=slot[:, k:k + 1], axis=0))\
                         .then_inc(g_in[k], 16)

            def w_stage(L, pairs):
                base, nb = L * nbm, pairs * 2
                with pool.Fori(0, pairs) as pair:
                    c = pair * 2
                    for k in range(2):
                        j = base + c
                        pool.wait_ge(mv_ok, done(j + k + 1))
                        pool.sem_inc(tick, 1)
                        g.tensor_scalar(var[:, k:k + 1], mv[:, k, 1:2], EPS, None, ALU.add).then_inc(var_ok, 1)
                        pool.wait_ge(var_ok, done(j + k + 1))
                        g.tensor_tensor(rstd[:, k:k + 1], var[:, k:k + 1], mhalf[:, :], ALU.pow).then_inc(rs_ok, 1)

            def stored(n):
                for k in range(2):
                    pool.wait_ge(h_st[k], 16 + n * 8)
                    pool.sem_inc(tick, 1)

            sum_stage(0, x, idx_x)
            w_stage(0, pairs_m)
            with pool.Fori(1, LAYERS - 1) as L:
                stored(L * nbm)
                sum_stage(L, hbuf, idx_h)
                w_stage(L, pairs_m)
            stored((LAYERS - 1) * nbm)
            sum_stage(LAYERS - 1, hbuf, idx_h)
            w_stage(LAYERS - 1, pairs_l)
            stored((LAYERS - 1) * nbm + nbl)
            IDX1 = 2 * NE + LAYERS * NE

            def gather(t, k, n):
                if not isinstance(t, int) or t > 0:
                    pool.wait_ge(f_sum, done(t + k - GS + 1))
                    pool.sem_inc(tick, 1)
                g.tensor_copy(slot[:, k:k + 1], idx_f[:, bass.ds(t + k, 1)]).then_inc(cp_idx, 1)
                pool.wait_ge(cp_idx, done(IDX1 + t + k + 1))
                pool.sem_inc(tick, 1)
                g.indirect_dma_start(out=hf[0:n, k, :], out_offset=None, in_=hbuf[:, :],
                                     in_offset=bass.IndirectOffsetOnAxis(ap=slot[0:n, k:k + 1], axis=0))\
                 .then_inc(hf_in[k], 16)

            def rstd_of(t, k, n):
                pool.wait_ge(f_mv, done(t + k + 1))
                pool.sem_inc(tick, 1)
                g.tensor_scalar(var[0:n, k:k + 1], mv[0:n, k, 1:2], EPS, None, ALU.add).then_inc(f_ve, 1)
                pool.wait_ge(f_ve, done(t + k + 1))
                g.tensor_tensor(rstd[0:n, k:k + 1], var[0:n, k:k + 1], mhalf[0:n, :], ALU.pow).then_inc(f_rs, 1)

            for s in (f_ve, f_rs):
                pool.sem_inc(s, PRIME)
            for k in range(GS):
                gather(0, k, P)
            with pool.Fori(0, (FLOOP - GS) // GS) as group:
                t = group * GS
                for k in range(GS):
                    rstd_of(t, k, P)
                    gather(t + GS, k, P)
            for k in range(GS):
                rstd_of(FLOOP - GS, k, P)
                if FLOOP + k <= FULL:
                    gather(FLOOP, k, P if FLOOP + k < FULL else TAIL)
            for k in range(FULL - FLOOP):
                rstd_of(FLOOP, k, P)
            rstd_of(FLOOP, FULL - FLOOP, TAIL)

        @block.vector
        def _(dve):
            v = nc.vector
            for s in (tg_cp, w_ok, b_ok, lo_ok, mv_ok, t_ok, u_ok, edge_ok, st_ok, f_sum, f_st, f_mv, f_o):
                dve.sem_inc(s, PRIME)
            steps = [0]

            def link(ins, *also):
                steps[0] += 1
                ins.then_inc(v_step, 1)
                dve.wait_ge(v_step, steps[0])

            link(v.memset(zero_bf, 0.0))
            link(v.memset(ones2[:, :].bitcast(f32), 1.0))
            link(v.memset(ntab, 0.0))
            link(v.memset(q0b, 0.0))
            link(v.memset(zcol[:, :], 0.0))
            dve.wait_ge(h_st[0], 16)
            dve.wait_ge(h_st[1], 16)
            for n, e in enumerate((src_i, dst_i)):
                link(v.tensor_scalar(hilo_i[:, 2 * n, :], e, 7, None, ALU.logical_shift_right))
                link(v.tensor_scalar(hilo_i[:, 2 * n + 1, :], e, P - 1, None, ALU.bitwise_and))
            link(v.tensor_copy(hilo, hilo_i))
            link(v.tensor_scalar(idx_x[:, 0:NE], src_i, float(N - 1), None, ALU.min))
            dve.wait_ge(p_step, 13)
            link(v.tensor_copy(iota[:, :], iota_i))
            for n, h in enumerate(hot):
                w = h.shape[2]
                v.tensor_tensor(h, iota[:, 0:w].unsqueeze(1).to_broadcast([P, NE, w]),
                                hilo[:, n, :].unsqueeze(2).to_broadcast([P, NE, w]), ALU.is_equal)\
                 .then_inc(hot_ok, 1)
            link(v.tensor_scalar(valid, node_i, float(N), None, ALU.is_lt))
            dve.wait_ge(hist_ok, 2)
            link(v.tensor_copy(outs, ps_s[0][0:NR, 0:P]))
            link(v.tensor_copy(ins, ps_s[1][0:NR, 0:P]))
            v.tensor_scalar(t1, outs, 1.0, None, ALU.max).then_inc(deg_ok, 1)
            v.tensor_scalar(t2, ins, 1.0, None, ALU.max).then_inc(deg_ok, 1)
            link(v.scalar_tensor_tensor(act_l, ins, 0.0, valid, ALU.is_gt, ALU.mult))
            link(v.scalar_tensor_tensor(act_m, outs, 0.0, act_l, ALU.is_gt, ALU.mult))
            link(v.tensor_tensor_scan(scan_l, ones_np, act_l, 0.0, ALU.mult, ALU.add))
            link(v.tensor_tensor_scan(scan_m, ones_np, act_m, 0.0, ALU.mult, ALU.add))
            v.tensor_copy(row_sums[:, 0:1], scan_l[:, P - 1:P]).then_inc(sums_ok, 1)
            v.tensor_copy(row_sums[:, 1:2], scan_m[:, P - 1:P]).then_inc(sums_ok, 1)
            dve.wait_ge(pre_ok, 2)
            link(v.tensor_copy(before, ps_s[0][0:NR, 0:2]))
            link(v.tensor_copy(totals, ps_s[1][:, 0:2]))
            c_last, c_mid = ntab[:, :, C_LAST], ntab[:, :, C_MID]
            link(v.scalar_tensor_tensor(c_last, scan_l, before[:, 0:1], act_l, ALU.add, ALU.subtract))
            link(v.scalar_tensor_tensor(c_mid, scan_m, before[:, 1:2], act_m, ALU.add, ALU.subtract))
            link(v.scalar_tensor_tensor(t3, c_mid, totals[0:NR, 1:2], act_l, ALU.subtract, ALU.mult))
            link(v.tensor_scalar(ntab[:, :, C_ROW], t3, totals[0:NR, 1:2], None, ALU.add))
            link(v.scalar_tensor_tensor(t3, c_last, totals[0:NR, 0:1], act_l, ALU.subtract, ALU.mult))
            v.tensor_scalar(fidx, t3, totals[0:NR, 0:1], None, ALU.add).then_inc(fid_ok, 1)
            dve.wait_ge(pow_ok, 2)
            link(v.tensor_copy(ntab[:, :, C_NOUT], t1))
            link(v.tensor_tensor(ntab[:, :, C_NIN], t2, valid, ALU.mult))
            link(v.tensor_tensor(ntab[:, :, C_NINM], t2, act_m, ALU.mult))
            v.engine_nop().then_inc(table_ok, 1)
            link(v.tensor_scalar(cnt_f, totals[0:1, :], float(2 * P), None, ALU.add))
            link(v.tensor_copy(cnt_i, cnt_f))
            link(v.tensor_scalar(cnt_i2, cnt_i, 8, None, ALU.logical_shift_right))
            link(v.tensor_scalar(counts[0:1, 0:1], cnt_i2[:, 1:2], 2.0, None, ALU.max))
            link(v.tensor_scalar(counts[0:1, 1:2], cnt_i2[:, 0:1], 2.0, None, ALU.max))
            dve.wait_ge(fidt_ok, 1)
            link(v.tensor_copy(idx_f[:, :], ps_s[0][:, 0:NR]))
            with dve.Fori(0, NE // GS) as group:
                i = group * GS
                for k in range(GS):
                    for got, one, kept in ((tg_d, dslot, dtab), (tg_s, sslot, stab)):
                        dve.wait_ge(got[k], i * 4 + 16)
                        dve.sem_inc(dve_tick, 1)
                        v.tensor_copy(kept[:, bass.ds(i + k, 1), :], one[:, k:k + 1, :]).then_inc(tg_cp, 1)
            dve.wait_ge(tg_cp, done(2 * NE))
            v.engine_nop().then_inc(kept_ok, 1)
            link(v.tensor_tensor(wgt_m[:, 0:NE], dtab[:, :, C_NINM], stab[:, :, C_NOUT], ALU.mult))
            link(v.tensor_tensor(wgt_l[:, 0:NE], dtab[:, :, C_NIN], stab[:, :, C_NOUT], ALU.mult))
            link(v.memset(wgt_m[:, NE:NE + 2], 0.0))
            link(v.memset(wgt_l[:, NE:NE + 2], 0.0))
            link(v.memset(rel_m[:, NE:NE + 2], 0.0))
            link(v.memset(rel_l[:, NE:NE + 2], 0.0))
            link(v.tensor_copy(idx_h[:, :], stab[:, :, C_ROW]))
            dve.wait_ge(pick_ok, 2)
            for n, (c, rel, q0) in enumerate(((C_MID, rel_m, q0_m), (C_LAST, rel_l, q0_l))):
                link(v.tensor_copy(q0b[:, n, 1:NE], ps_s[n][:, 0:NE - 1]))
                link(v.tensor_tensor(rel[:, 0:NE], dtab[:, :, c], q0b[:, n, :], ALU.subtract))
                link(v.tensor_copy(q0[:, :], q0b[0:1, n, :]))
            v.engine_nop().then_inc(setup_ok, 1)
            pairs_m, pairs_l, nbm, nbl = tile_counts(dve)

            SB = NE + 2

            def select(L, i, k, rel, wgt):
                v.tensor_scalar(sel[:, k % 2, :], iota[:, :], rel[:, bass.ds(i, 1)], wgt[:, bass.ds(i, 1)],
                                ALU.is_equal, ALU.mult).then_inc(sel_ok, 1)

            def zero_tail(nb):
                v.tensor_copy(agg_t[:, :, bass.ds((nb - 2) * P, 2 * P)],
                              zcol[:, :].unsqueeze(2).to_broadcast([P, KB, 2 * P])).then_inc(v_tail, 1)

            def sum_stage(L, rel, wgt, q0):
                base = L * nbm
                dve.wait_ge(hi_ok, done(base))
                dve.sem_inc(dve_tick, 1)
                v.memset(agg_t[:, :, 0:1], 0.0).then_inc(zero_ok, 1)
                for k in range(2):
                    select(L, k, k, rel, wgt)
                for q in range(KB):
                    with dve.Fori((q * EDGE_TILES_PER_CHUNK) // GS, ((q + 1) * EDGE_TILES_PER_CHUNK) // GS) as group:
                        t = group * GS
                        for k in range(GS):
                            i = L * NE + t
                            r0 = dve.value_load(q0[0:1, bass.ds(t + k, 1)], min_val=0, max_val=N)
                            dve.wait_ge(ev_ok, done(i + k))
                            dve.wait_ge(edge_ok, done(i + k))
                            dve.sem_inc(dve_tick, 1)
                            dve.wait_ge(agg_ok, done(i + k + 1))
                            col = agg_t[:, :, bass.ds(r0, 1)]
                            v.tensor_tensor(col, ps_a[k % 2][:, :, 0:1], col, ALU.add).then_inc(edge_ok, 1)
                            select(L, t + k + 2, k, rel, wgt)
                    if q == 0:
                        dve.wait_ge(y_ok, done(base))
                        dve.sem_inc(dve_tick, 1)
                    dve.wait_ge(raw_in[q % 2], (L * 2 + q // 2 + 1) * 16)
                    dve.sem_inc(dve_tick, 1)
                    v.tensor_copy(w_hi[:, q, :], w_raw[:, q % 2, :]).then_inc(wh_ok, 1)
                    dve.wait_ge(wh_ok, L * KB + q + 1)
                    v.tensor_tensor(w_lo[:, q, :], w_raw[:, q % 2, :], w_hi[:, q, :].bitcast(f32), ALU.subtract)\
                     .then_inc(w_ok, 1)
                dve.wait_ge(b_in, (L + 1) * 16)
                dve.sem_inc(dve_tick, 1)
                v.tensor_copy(b_high, b_raw[0:2, 0, :]).then_inc(bh_ok, 1)
                dve.wait_ge(bh_ok, L + 1)
                v.scalar_tensor_tensor(b_rows[:, :], b_high.bitcast(f32), negm[:, :], b_raw[0:2, 0, :],
                                       ALU.mult, ALU.add).then_inc(b_ok, 1)

            def low(j, c, k):
                dve.wait_ge(hi_ok, done(j + 1))
                v.tensor_tensor(s_lo[:, k, :, :], agg_t[:, :, bass.ds(c * P, P)], s_hi[:, k, :, :].bitcast(f32),
                                ALU.subtract).then_inc(lo_ok, 1)

            def norm(j, k):
                dve.wait_ge(y_ok, done(j + 1))
                v.bn_stats(stats[:, k, :], ps_y[k][:, :]).then_inc(st_ok, 1)
                dve.wait_ge(st_ok, done(j + 1))
                dve.sem_inc(dve_tick, 1)
                v.bn_aggr(mv[:, k, :], stats[:, k, :]).then_inc(mv_ok, 1)
                dve.wait_ge(h_ok, done(j - 1))
                dve.wait_ge(mv_ok, done(j + 1))
                dve.sem_inc(dve_tick, 1)
                v.scalar_tensor_tensor(rows[:, k, :], ps_y[k][:, :], mv[:, k, 0:1], gam[:, :],
                                       ALU.subtract, ALU.mult).then_inc(t_ok, 1)
                dve.wait_ge(t_ok, done(j + 1))
                dve.sem_inc(dve_tick, 1)
                dve.wait_ge(rs_ok, done(j + 1))
                v.scalar_tensor_tensor(rows[:, k, :], rows[:, k, :], rstd[:, k:k + 1], bet[:, :],
                                       ALU.mult, ALU.add).then_inc(u_ok, 1)

            def w_stage(L, pairs):
                base, nb = L * nbm, pairs * 2
                low(base, 0, 0)
                dve.wait_ge(gb_in, (L + 1) * 32)
                dve.sem_inc(dve_tick, 1)
                with dve.Fori(0, pairs - 1) as pair:
                    c = pair * 2
                    for k in range(2):
                        j = base + c
                        low(j + k + 1, c + k + 1, 1 - k)
                        norm(j + k, k)
                low(base + nb - 1, nb - 1, 1)
                norm(base + nb - 2, 0)
                norm(base + nb - 1, 1)

            zero_tail(nbm)
            with dve.Fori(0, LAYERS - 1) as L:
                sum_stage(L, rel_m, wgt_m, q0_m)
                w_stage(L, pairs_m)
            dve.wait_ge(hi_ok, done((LAYERS - 1) * nbm))
            dve.sem_inc(dve_tick, 1)
            zero_tail(nbl)
            sum_stage(LAYERS - 1, rel_l, wgt_l, q0_l)
            w_stage(LAYERS - 1, pairs_l)

            def last(t, k, n):
                dve.wait_ge(xf_in[k], (t // GS + 1) * 16 if isinstance(t, int) else t * 4 + 16)
                dve.sem_inc(dve_tick, 1)
                dve.wait_ge(hf_in[k], (t // GS + 1) * 16 if isinstance(t, int) else t * 4 + 16)
                dve.sem_inc(dve_tick, 1)
                v.tensor_tensor(xs[0:n, k, :], xs[0:n, k, :], hf[0:n, k, :], ALU.add).then_inc(f_sum, 1)
                dve.wait_ge(f_sum, done(t + k + 1))
                v.bn_stats(stats[0:n, k, :], xs[0:n, k, :]).then_inc(f_st, 1)
                dve.wait_ge(f_st, done(t + k + 1))
                dve.sem_inc(dve_tick, 1)
                v.bn_aggr(mv[0:n, k, :], stats[0:n, k, :]).then_inc(f_mv, 1)
                dve.wait_ge(f_rs, done(t + k + 1))
                dve.sem_inc(dve_tick, 1)
                v.tensor_scalar(of[0:n, k, :], xs[0:n, k, :], mv[0:n, k, 0:1], rstd[0:n, k:k + 1],
                                ALU.subtract, ALU.mult).then_inc(f_o, 1)

            for k in range(GS):
                last(0, k, P)
            with dve.Fori(1, FLOOP // GS) as group:
                t = group * GS
                for k in range(GS):
                    dve.wait_ge(o_st[k], t * 4)
                    dve.sem_inc(dve_tick, 1)
                    last(t, k, P)
            for k in range(FULL - FLOOP + 1):
                dve.wait_ge(o_st[k], FLOOP * 4)
                last(FLOOP, k, P if FLOOP + k < FULL else TAIL)

        @block.scalar
        def _(act):
            a = nc.scalar
            for s in (ev_ok, hi_ok, h_ok):
                act.sem_inc(s, PRIME)
            pairs_m, pairs_l, nbm, nbl = tile_counts(act)

            def hold(s, n):
                act.wait_ge(s, n)
                act.sem_inc(act_tick, 1)

            def sum_stage(L, q0):
                hold(lo_ok, done(L * nbm))
                with act.Fori(0, NE // GS) as group:
                    t = group * GS
                    for k in range(GS):
                        i = L * NE + t
                        r0 = act.value_load(q0[0:1, bass.ds(t + k, 1)], min_val=0, max_val=N)
                        hold(agg_ok, done(i + k + 1))
                        hold(edge_ok, done(i + k + 1))
                        a.activation(agg_t[:, :, bass.ds(r0 + 1, P - 1)], ps_a[k % 2][:, :, 1:P], ACT.Copy)\
                         .then_inc(ev_ok, 1)

            def high(j, c, k):
                hold(y_ok, done(j - 1))
                a.activation(s_hi[:, k, :, :], agg_t[:, :, bass.ds(c * P, P)], ACT.Copy).then_inc(hi_ok, 1)

            def gelu(j, j_pair, k):
                hold(u_ok, done(j + 1))
                hold(h_st[k], j_pair * 8 + 16)
                a.activation(rows[:, 2 + k, :], rows[:, k, :], ACT.Gelu).then_inc(h_ok, 1)

            def w_stage(L, pairs):
                base, nb = L * nbm, pairs * 2
                hold(edge_ok, done(L * NE + NE))
                hold(ev_ok, done(L * NE + NE))
                hold(b_ok, done(L + 1))
                high(base, 0, 0)
                high(base + 1, 1, 1)
                with act.Fori(0, pairs - 1) as pair:
                    c = pair * 2
                    for k in range(2):
                        j = base + c
                        high(j + k + 2, c + k + 2, k)
                        gelu(j + k, j, k)
                for k in range(2):
                    gelu(base + nb - 2 + k, base + nb - 2, k)

            with act.Fori(0, LAYERS - 1) as L:
                sum_stage(L, q0_m)
                w_stage(L, pairs_m)
            sum_stage(LAYERS - 1, q0_l)
            w_stage(LAYERS - 1, pairs_l)

        @block.tensor
        def _(pe):
            mm = nc.tensor.matmul
            for s in (agg_ok, y_ok):
                pe.sem_inc(s, PRIME)
            pe.wait_ge(hot_ok, 4)
            for n in range(2):
                acc = ps_s[n][0:NR, 0:P]
                mm(acc, zero_bf[:, 0:NR], zero_bf, start=True, stop=False)
                with pe.Fori(0, NE) as i:
                    mm(acc, hot[2 * n][:, bass.ds(i, 1), :].rearrange("p a b -> p (a b)"),
                       hot[2 * n + 1][:, bass.ds(i, 1), :].rearrange("p a b -> p (a b)"), start=False, stop=False)
                mm(acc, zero_bf[:, 0:NR], zero_bf, start=False, stop=True).then_inc(hist_ok, 1)
            pe.wait_ge(sums_ok, 2)
            mm(ps_s[0][0:NR, 0:2], lower, row_sums, start=True, stop=True).then_inc(pre_ok, 1)
            mm(ps_s[1][:, 0:2], ones_np, row_sums, start=True, stop=True).then_inc(pre_ok, 1)
            pe.wait_ge(fid_ok, 1)
            nc.tensor.transpose(ps_s[0][:, 0:NR], fidx, ident[0:NR, 0:NR]).then_inc(fidt_ok, 1)
            pe.wait_ge(kept_ok, 1)
            mm(ps_s[0][:, 0:NE], pick, dtab[:, :, C_MID], start=True, stop=True).then_inc(pick_ok, 1)
            mm(ps_s[1][:, 0:NE], pick, dtab[:, :, C_LAST], start=True, stop=True).then_inc(pick_ok, 1)
            pairs_m, pairs_l, nbm, nbl = tile_counts(pe)

            def sum_stage(L):
                with pe.Fori(0, NE // GS) as group:
                    t = group * GS
                    for k in range(GS):
                        i = L * NE + t
                        pe.wait_ge(g_in[k], i * 4 + 16)
                        pe.wait_ge(sel_ok, i + L * 2 + k + 1)
                        pe.sem_inc(pe_tick, 1)
                        pe.wait_ge(ev_ok, done(i + k - 1))
                        pe.wait_ge(edge_ok, done(i + k - 1))
                        pe.sem_inc(pe_tick, 1)
                        for b in range(KB):
                            m = mm(ps_a[k % 2][:, b, :], rows[:, k, b * P:(b + 1) * P], sel[:, k % 2, :],
                                   start=True, stop=True)
                        m.then_inc(agg_ok, 1)

            def w_stage(L, pairs):
                base, nb = L * nbm, pairs * 2
                pe.wait_ge(w_ok, done(L * KB + KB))
                pe.sem_inc(pe_tick, 1)
                pe.wait_ge(b_ok, done(L + 1))
                pe.sem_inc(pe_tick, 1)
                with pe.Fori(0, pairs) as pair:
                    c = pair * 2
                    for k in range(2):
                        j = base + c
                        pe.wait_ge(lo_ok, done(j + k + 1))
                        pe.sem_inc(pe_tick, 1)
                        pe.wait_ge(t_ok, done(j + k - 1))
                        pe.sem_inc(pe_tick, 1)
                        mm(ps_y[k][:, :], ones2[:, :], b_rows[:, :], start=True, stop=False)
                        for b in range(KB):
                            for s, w in ((s_hi, w_hi), (s_hi, w_lo), (s_lo, w_hi)):
                                last = s is s_lo and b == KB - 1
                                m = mm(ps_y[k][:, :], s[:, k, b, :], w[:, b, :], start=False, stop=last)
                        m.then_inc(y_ok, 1)

            with pe.Fori(0, LAYERS - 1) as L:
                sum_stage(L)
                w_stage(L, pairs_m)
            sum_stage(LAYERS - 1)
            w_stage(LAYERS - 1, pairs_l)


def kernel(x, src, dst, L0_gnn_Ws, L0_gnn_bs, L0_gnn_ln_g, L0_gnn_ln_b):
    import numpy as np
    import concourse.bacc as bacc
    from concourse.bass_utils import run_bass_kernel_spmd as run

    def tiles(e):
        flat = np.full(NE * ET, N, e.dtype)
        flat[:E] = e
        laid = np.full((P, NE), N, e.dtype)
        laid[:ET] = flat.reshape(NE, ET).T
        return laid

    arrays = {"in_x": np.ascontiguousarray(x), "in_src": tiles(np.asarray(src)), "in_dst": tiles(np.asarray(dst)),
              "in_Ws": np.ascontiguousarray(L0_gnn_Ws), "in_bs": np.ascontiguousarray(L0_gnn_bs),
              "in_ln_g": np.ascontiguousarray(L0_gnn_ln_g), "in_ln_b": np.ascontiguousarray(L0_gnn_ln_b)}
    nc = bacc.Bacc("TRN2", target_bir_lowering=False, num_devices=1)
    args = [nc.dram_tensor(k, v.shape, mybir.dt.from_np(v.dtype), kind="ExternalInput").ap()
            for k, v in arrays.items()]
    args.append(nc.dram_tensor("out_0", (N, D), f32, kind="ExternalOutput").ap())
    build(nc, *args)
    return run(nc, [arrays], core_ids=[0]).results[0]["out_0"]
```

```python
import concourse.bass as bass
from concourse import mybir
from contextlib import ExitStack

N = 10000
E = 10000
D = 512
LAYERS = 8
EPS = 1e-5
P = 128
KB = D // P
ET = P - 1
NE = 80
NR = 80
PADDED = NR * P
GS = 5
UN = 2 * GS
FS = 4
COLS = 8
C_LAST, C_MID, C_NIN, C_NINM, C_NOUT, C_ROW = range(6)
PRIME = 8

f32, f32r, i32, bf16 = mybir.dt.float32, mybir.dt.float32r, mybir.dt.int32, mybir.dt.bfloat16
ALU = mybir.AluOpType
ACT = mybir.ActivationFunctionType


def done(n):
    return n + PRIME


def build(nc, x, src, dst, Ws, bs, ln_g, ln_b, out):
    hbuf = nc.dram_tensor("h_rows", (PADDED, D), f32).ap()
    ntab_d = nc.dram_tensor("node_table", (PADDED, COLS), f32).ap()
    edges_d = nc.dram_tensor("edges_needed_first", (NE * ET, 4), f32).ap()
    ctx = ExitStack()
    with ctx:
        def sb(n, s, d=f32):
            return ctx.enter_context(nc.sbuf_tensor(n, s, d))

        def sem(n):
            return ctx.enter_context(nc.semaphore(n))

        agg_t = sb("agg_t", [P, KB, PADDED])
        w_hi = sb("w_hi", [P, KB, D], f32r)
        w_lo = sb("w_lo", [P, KB, D], f32r)
        w_raw = sb("w_raw", [P, 2, D])
        b_rows = sb("b_rows", [2, D], f32r)
        zcol = sb("zcol", [P, KB])
        b_raw = w_raw
        bet = sb("bet", [P, D])
        s_hi = sb("s_hi", [P, 2, KB, P], f32r)
        s_lo = sb("s_lo", [P, 2, KB, P], f32r)
        b_high = s_hi[0:2, 0, :, :].rearrange("p a b -> p (a b)")
        rows = sb("rows", [P, GS, D])
        gam = rows[:, 4, :]
        sel = sb("sel", [P, 2, P])
        iota = sb("iota", [P, P])
        ones2 = sb("ones2", [2, P], f32r)
        negm = sb("negm", [2, 1])
        idx_now = sb("idx_now", [P, NE + GS], i32)
        idx_h = sb("idx_h", [P, NE + GS], i32)
        idx_l = sb("idx_l", [P, NE + GS], i32)
        idx_f = sb("idx_f", [P, NR], i32)
        wgt_m = sb("wgt_m", [P, NE + 2])
        wgt_l = sb("wgt_l", [P, NE + 2])
        rel_m = sb("rel_m", [P, NE + 2])
        rel_l = sb("rel_l", [P, NE + 2])
        q0_m = sb("q0_m", [1, NE], i32)
        q0_l = sb("q0_l", [1, NE], i32)
        counts = sb("counts", [1, 3], i32)
        slot = sb("slot", [P, UN], i32)
        slot2 = sb("slot2", [P, 2 * FS], i32)
        stats = sb("stats", [P, FS, 6])
        mv = sb("mv", [P, FS, 2])
        var = sb("var", [P, FS])
        rstd = sb("rstd", [P, FS])
        mhalf = sb("mhalf", [P, 1])

        ps_a = [ctx.enter_context(nc.psum_tensor(f"ps_a{i}", [P, KB, P], f32)) for i in range(GS)]
        ps_y = [ctx.enter_context(nc.psum_tensor(f"ps_y{i}", [P, D], f32)) for i in range(2)]
        ps_s = [ps_a[i][:, :, :].rearrange("p k n -> p (k n)") for i in range(4)]

        class Space:
            at = 0

        def part(shape, d=f32):
            size = 1
            for v in shape[1:]:
                size *= v
            words = size * (2 if d is bf16 else 4) // 4
            flat = agg_t[:, :, :].rearrange("p k n -> p (k n)")[0:shape[0], Space.at:Space.at + words]
            Space.at += words
            if d is not f32:
                flat = flat.bitcast(d)
            if len(shape) == 3:
                flat = flat.rearrange("p (a b) -> p a b", b=shape[2])
            return flat

        src_i = part([P, NE], i32)
        dst_i = part([P, NE], i32)
        hilo_i = part([P, 4, NE], i32)
        hilo = part([P, 4, NE], bf16)
        iota_b = part([P, P], bf16)
        hot = [part([P, NE, n], bf16) for n in (NR, P, NR, P)]
        zero_bf = part([P, P], bf16)
        zero_row = part([P, D])
        node_i = part([NR, P], i32)
        iota_i = part([P, P], i32)
        valid = part([NR, P])
        outs, ins = part([NR, P]), part([NR, P])
        act_l, act_m = part([NR, P]), part([NR, P])
        row_sums = part([NR, 2])
        scan_l, scan_m = part([NR, P]), part([NR, P])
        before = part([NR, 2])
        totals = part([P, 2])
        ones = part([P, P])
        ones_np = ones[0:NR, :]
        before_p = part([P, P])
        lower = before_p[0:NR, 0:NR]
        ntab = part([NR, P, COLS])
        t1, t2, t3 = part([NR, P]), part([NR, P]), part([NR, P])
        r1, r2 = part([NR, P]), part([NR, P])
        fidx = part([NR, P])
        ident = part([P, P])
        pick = part([P, P])
        dtab = part([P, NE, COLS])
        stab = part([P, NE, COLS])
        dslot = part([P, FS, COLS])
        sslot = part([P, FS, COLS])
        q0b = part([P, 2, NE])
        keep, col_sum, col_scan, pos, other = [part([P, NE]) for _ in range(5)]
        edge_i, target = part([P, NE], i32), part([P, NE], i32)
        pay = part([P, NE, 4])
        em = part([P, NE, 4])
        pay_slot = part([P, 2 * FS, 4])
        limits = part([1, NE // UN])
        its_f = part([1, 1])
        cnt_f, cnt_i, cnt_i2 = part([1, 2]), part([1, 2], i32), part([1, 2], i32)
        Space.at = 0
        xs = part([P, FS, D])
        hf = part([P, FS, D])
        of = part([P, FS, D])

        hot_ok = sem("one_hots_made")
        hist_ok = sem("histograms_done")
        deg_ok = sem("degrees_clipped")
        pow_ok = sem("norms_made")
        sums_ok = sem("row_sums_made")
        pre_ok = sem("prefix_done")
        fid_ok = sem("final_index_made")
        fidt_ok = sem("final_index_transposed")
        table_ok = sem("node_table_made")
        pick_ok = sem("first_ranks_spread")
        keep_ok = sem("needed_edges_marked")
        place_ok = sem("places_summed")
        pay_ok = sem("edges_in_slots")
        sc_st = [sem(f"edges_scattered{k}") for k in range(2)]
        em_in = sem("needed_edges_in")
        v_step = sem("vector_steps")
        p_step = sem("pool_setup_steps")
        rows_clear = sem("zero_row_made")
        h_clear = sem("h_cleared")
        nt_st = sem("node_table_stored")
        tick = sem("pool_ticks")
        cp_idx = sem("index_copied")
        tg_d = [sem(f"dst_row_in{k}") for k in range(FS)]
        tg_s = [sem(f"src_row_in{k}") for k in range(FS)]
        tg_cp = sem("table_rows_kept")
        setup_ok = sem("setup_done")
        g_in = [sem(f"rows_gathered{k}") for k in range(GS)]
        sel_ok = sem("selection_made")
        ix_ok = sem("gather_indices_ready")
        now_ok = sem("indices_switched")
        agg_ok = sem("tile_summed")
        ev_ok = sem("sums_kept")
        edge_ok = sem("first_column_added")
        raw_in = [sem(f"w_chunk_in{k}") for k in range(2)]
        b_in = sem("bias_in")
        gb_in = sem("gamma_beta_in")
        w_ok = sem("w_chunk_split")
        b_ok = sem("bias_split")
        hi_ok = sem("high_half_made")
        lo_ok = sem("low_half_made")
        y_ok = sem("product_done")
        st_ok = sem("stats_made")
        act_tick = sem("act_ticks")
        dve_tick = sem("dve_ticks")
        mv_ok = sem("mean_var_made")
        var_ok = sem("var_eps_made")
        rs_ok = sem("rstd_made")
        t_ok = sem("centred")
        u_ok = sem("normalised")
        h_ok = sem("gelu_done")
        h_st = [sem(f"h_stored{k}") for k in range(2)]
        pe_tick = sem("pe_ticks")
        sp_tick = sem("sp_ticks")
        wh_ok = sem("w_high_made")
        bh_ok = sem("bias_high_made")
        v_tail = sem("tail_cleared")
        zero_ok = sem("column_cleared")
        xf_in = [sem(f"x_tile_in{k}") for k in range(FS)]
        hf_in = [sem(f"h_tile_in{k}") for k in range(FS)]
        f_sum = sem("residual_added")
        f_st = sem("final_stats")
        f_mv = sem("final_mean_var")
        f_ve = sem("final_var_eps")
        f_rs = sem("final_rstd")
        f_o = sem("final_rows_made")
        o_st = [sem(f"out_stored{k}") for k in range(FS)]
        o_last = sem("out_tail_stored")

        block = ctx.enter_context(nc.Block())

        def tile_counts(eng):
            eng.wait_ge(setup_ok, 1)
            mid = eng.value_load(counts[0:1, 0:1], min_val=0, max_val=NR // 2 - 3) + 3
            last = eng.value_load(counts[0:1, 1:2], min_val=0, max_val=NR // 2 - 3) + 3
            its = eng.value_load(counts[0:1, 2:3], min_val=0, max_val=NE // UN - 4) + 4
            return mid, last, mid * 2, last * 2, its, its * UN

        FULL = N // P
        TAIL = N - FULL * P
        FLOOP = FULL // FS * FS

        @block.sync
        def _(sp):
            sp.dma_start(src_i, src).then_inc(h_st[0], 16)
            sp.dma_start(dst_i, dst).then_inc(h_st[1], 16)
            sp.wait_ge(rows_clear, 1)
            sp.dma_start(hbuf.rearrange("(a p) n -> p a n", p=P),
                         zero_row.unsqueeze(1).to_broadcast([P, NR, D])).then_inc(h_clear, 16)
            sp.wait_ge(table_ok, 1)
            sp.dma_start(ntab_d.rearrange("(a b) c -> a b c", b=P), ntab).then_inc(nt_st, 16)
            for k in range(2):
                sp.wait_ge(sc_st[k], NE // 2 * 16)
            sp.dma_start(em[0:ET, :, :], edges_d[0:NE * ET, :].rearrange("(t p) c -> p t c", p=ET)).then_inc(em_in, 16)
            sp.wait_ge(h_clear, 16)
            pairs_m, pairs_l, nbm, nbl, its_m, nem = tile_counts(sp)

            def layer(L, pairs, ne):
                base = L * nbm
                for q in range(KB):
                    sp.wait_ge(w_ok, done(L * KB + q - 1))
                    sp.sem_inc(sp_tick, 1)
                    if q == 0:
                        sp.wait_ge(b_ok, done(L))
                        sp.sem_inc(sp_tick, 1)
                    sp.dma_start(w_raw[:, q % 2, :], Ws[bass.ds(L, 1), q * P:(q + 1) * P, :]
                                 .rearrange("a p n -> p (a n)")).then_inc(raw_in[q % 2], 16)
                sp.wait_ge(w_ok, done(L * KB + KB))
                sp.sem_inc(sp_tick, 1)
                sp.dma_start(b_raw[0:2, 0, :], bs[bass.ds(L, 1), :].rearrange("a n -> (a n)")
                             .partition_broadcast(2)).then_inc(b_in, 16)
                sp.wait_ge(u_ok, done(base))
                sp.sem_inc(sp_tick, 1)
                sp.wait_ge(agg_ok, done(L * nem + ne))
                sp.sem_inc(sp_tick, 1)
                sp.dma_start(gam, ln_g[bass.ds(L, 1), :].rearrange("a n -> (a n)")
                             .partition_broadcast(P)).then_inc(gb_in, 16)
                sp.dma_start(bet[:, :], ln_b[bass.ds(L, 1), :].rearrange("a n -> (a n)")
                             .partition_broadcast(P)).then_inc(gb_in, 16)
                with sp.Fori(0, pairs) as pair:
                    c = pair * 2
                    for k in range(2):
                        j = base + c
                        sp.wait_ge(h_ok, done(j + k + 1))
                        sp.sem_inc(sp_tick, 1)
                        sp.dma_start(hbuf[bass.ds((c + k) * P, P), :], rows[:, 2 + k, :])\
                          .then_inc(h_st[k], 16)

            with sp.Fori(0, LAYERS - 1) as L:
                layer(L, pairs_m, nem)
            layer(LAYERS - 1, pairs_l, NE)
            sp.wait_ge(lo_ok, done((LAYERS - 1) * nbm + nbl))
            sp.sem_inc(sp_tick, 1)

            def load(t, k, n):
                if not isinstance(t, int):
                    sp.wait_ge(f_o, done(t + k - FS + 1))
                    sp.sem_inc(sp_tick, 1)
                sp.dma_start(xs[0:n, k, :], x[bass.ds((t + k) * P, n), :]).then_inc(xf_in[k], 16)

            def store(t, k, n):
                sp.wait_ge(f_o, done(t + k + 1))
                sp.sem_inc(sp_tick, 1)
                sp.dma_start(out[bass.ds((t + k) * P, n), :], of[0:n, k, :])\
                  .then_inc(o_st[k] if n == P else o_last, 16)

            for k in range(FS):
                load(0, k, P)
            with sp.Fori(0, (FLOOP - FS) // FS) as group:
                t = group * FS
                for k in range(FS):
                    store(t, k, P)
                    load(t + FS, k, P)
            for k in range(FS):
                store(FLOOP - FS, k, P)
                if FLOOP + k < FULL:
                    sp.dma_start(xs[:, k, :], x[(FLOOP + k) * P:(FLOOP + k + 1) * P, :]).then_inc(xf_in[k], 16)
                elif FLOOP + k == FULL:
                    sp.dma_start(xs[0:TAIL, k, :], x[FULL * P:N, :]).then_inc(xf_in[k], 16)
            for k in range(FULL - FLOOP):
                store(FLOOP, k, P)
            store(FLOOP, FULL - FLOOP, TAIL)
            for k in range(FS):
                sp.wait_ge(o_st[k], 16 * (FLOOP // FS + (FLOOP + k < FULL)))
            sp.wait_ge(o_last, 16)

        @block.gpsimd
        def _(pool):
            g = nc.gpsimd
            for s in (rs_ok, var_ok, cp_idx, lo_ok):
                pool.sem_inc(s, PRIME)
            g.memset(zero_row, 0.0).then_inc(rows_clear, 1)
            g.iota(node_i, pattern=[[1, P]], base=0, channel_multiplier=P).then_inc(p_step, 1)
            g.iota(iota_i, pattern=[[1, P]], base=0, channel_multiplier=0).then_inc(p_step, 1)
            g.memset(mhalf[:, :], -0.5).then_inc(p_step, 1)
            g.memset(ones, 1.0).then_inc(p_step, 1)
            g.memset(before_p, 1.0).then_inc(p_step, 1)
            g.iota(edge_i, pattern=[[ET, NE]], base=0, channel_multiplier=1).then_inc(p_step, 1)
            g.memset(ident, 0.0).then_inc(p_step, 1)
            g.memset(pick, 1.0).then_inc(p_step, 1)
            g.memset(negm[:, :], -1.0).then_inc(p_step, 1)
            pool.wait_ge(p_step, 9)
            g.affine_select(out=before_p, in_=before_p, compare_op=ALU.is_gt, fill=0.0, base=0,
                            pattern=[[1, P]], channel_multiplier=-1).then_inc(p_step, 1)
            g.affine_select(out=ident, in_=ident, compare_op=ALU.not_equal, fill=1.0, base=0,
                            pattern=[[-1, P]], channel_multiplier=1).then_inc(p_step, 1)
            g.affine_select(out=pick, in_=pick, compare_op=ALU.is_equal, fill=0.0, base=-(ET - 1),
                            pattern=[[0, P]], channel_multiplier=1).then_inc(p_step, 1)
            g.affine_select(out=negm[:, :], in_=negm[:, :], compare_op=ALU.not_equal, fill=0.0, base=0,
                            pattern=[[0, 1]], channel_multiplier=1).then_inc(p_step, 1)
            pool.wait_ge(nt_st, 16)
            with pool.Fori(0, NE // (2 * FS)) as group:
                i = group * (2 * FS)
                for half in range(2):
                    own = slice(half * FS, half * FS + FS)
                    pool.wait_ge(tg_cp, done(2 * (i + (half - 1) * FS)))
                    pool.sem_inc(tick, 1)
                    g.tensor_copy(slot[:, own], dst_i[:, bass.ds(i + half * FS, FS)]).then_inc(cp_idx, 1)
                    g.tensor_copy(slot2[:, own], src_i[:, bass.ds(i + half * FS, FS)]).then_inc(cp_idx, 1)
                    pool.wait_ge(cp_idx, done(group * 4 + half * 2 + 2))
                    pool.sem_inc(tick, 1)
                    for k in range(FS):
                        n = half * FS + k
                        pool.wait_ge(tg_cp, done(2 * (i + n - FS + 1)))
                        pool.sem_inc(tick, 1)
                        g.indirect_dma_start(out=dslot[:, k, :], out_offset=None, in_=ntab_d[:, :],
                                             in_offset=bass.IndirectOffsetOnAxis(ap=slot[:, n:n + 1], axis=0))\
                         .then_inc(tg_d[k], 16)
                        g.indirect_dma_start(out=sslot[:, k, :], out_offset=None, in_=ntab_d[:, :],
                                             in_offset=bass.IndirectOffsetOnAxis(ap=slot2[:, n:n + 1], axis=0))\
                         .then_inc(tg_s[k], 16)
            with pool.Fori(0, NE // (2 * FS)) as group:
                for half in range(2):
                    pool.wait_ge(pay_ok, group * 4 + half * 2 + 2)
                    pool.sem_inc(tick, 1)
                    for k in range(half * FS, half * FS + FS):
                        g.indirect_dma_start(out=edges_d[:, :],
                                             out_offset=bass.IndirectOffsetOnAxis(ap=slot2[0:ET, k:k + 1], axis=0),
                                             in_=pay_slot[0:ET, k, :], in_offset=None).then_inc(sc_st[half], 16)
            pairs_m, pairs_l, nbm, nbl, its_m, nem = tile_counts(pool)

            def sum_stage(L, table, its):
                with pool.Fori(0, its) as group:
                    i = L * nem + group * UN
                    for k in range(UN):
                        if k % GS == 0:
                            pool.wait_ge(ix_ok, L * (its_m * 2 + 1) + group * 2 + k // GS + 1)
                            pool.sem_inc(tick, 1)
                        pool.wait_ge(agg_ok, done(i + k - GS + 1))
                        pool.sem_inc(tick, 1)
                        g.indirect_dma_start(out=rows[:, k % GS, :], out_offset=None, in_=table[:, :],
                                             in_offset=bass.IndirectOffsetOnAxis(ap=slot[:, k:k + 1], axis=0))\
                         .then_inc(g_in[k % GS], 16)

            def low(j, c, k):
                pool.wait_ge(hi_ok, done(j + 1))
                pool.sem_inc(tick, 1)
                g.tensor_tensor(s_lo[:, k, :, :], agg_t[:, :, bass.ds(c * P, P)], s_hi[:, k, :, :].bitcast(f32),
                                ALU.subtract).then_inc(lo_ok, 1)

            def inverse(j, k):
                pool.wait_ge(mv_ok, done(j + 1))
                pool.sem_inc(tick, 1)
                g.tensor_scalar(var[:, k:k + 1], mv[:, k, 1:2], EPS, None, ALU.add).then_inc(var_ok, 1)
                pool.wait_ge(var_ok, done(j + 1))
                g.tensor_tensor(rstd[:, k:k + 1], var[:, k:k + 1], mhalf[:, :], ALU.pow).then_inc(rs_ok, 1)

            def w_stage(L, pairs):
                base, nb = L * nbm, pairs * 2
                low(base, 0, 0)
                low(base + 1, 1, 1)
                with pool.Fori(0, pairs - 1) as pair:
                    c = pair * 2
                    for k in range(2):
                        low(base + c + k + 2, c + k + 2, k)
                        inverse(base + c + k, k)
                inverse(base + nb - 2, 0)
                inverse(base + nb - 1, 1)

            def stored(n):
                for k in range(2):
                    pool.wait_ge(h_st[k], 16 + n * 8)
                    pool.sem_inc(tick, 1)

            sum_stage(0, x, its_m)
            w_stage(0, pairs_m)
            with pool.Fori(1, LAYERS - 1) as L:
                stored(L * nbm)
                sum_stage(L, hbuf, its_m)
                w_stage(L, pairs_m)
            stored((LAYERS - 1) * nbm)
            sum_stage(LAYERS - 1, hbuf, NE // UN)
            w_stage(LAYERS - 1, pairs_l)
            stored((LAYERS - 1) * nbm + nbl)
            IDX1 = 2 * NE // FS

            def indices(t, half):
                g.tensor_copy(slot2[:, half * FS:half * FS + FS], idx_f[:, bass.ds(t, FS)]).then_inc(cp_idx, 1)
                pool.wait_ge(cp_idx, done(IDX1 + t // FS + 1) if isinstance(t, int) else done(IDX1 + 1) + t // FS)
                pool.sem_inc(tick, 1)

            def gather(t, k, n, half):
                if not isinstance(t, int) or t > 0:
                    pool.wait_ge(f_sum, done(t + k - FS + 1))
                    pool.sem_inc(tick, 1)
                g.indirect_dma_start(out=hf[0:n, k, :], out_offset=None, in_=hbuf[:, :],
                                     in_offset=bass.IndirectOffsetOnAxis(
                                         ap=slot2[0:n, half * FS + k:half * FS + k + 1], axis=0))\
                 .then_inc(hf_in[k], 16)

            def rstd_of(t, k, n):
                pool.wait_ge(f_ve, done(t + k + 1))
                g.tensor_tensor(rstd[0:n, k:k + 1], var[0:n, k:k + 1], mhalf[0:n, :], ALU.pow).then_inc(f_rs, 1)

            pool.sem_inc(f_rs, PRIME)
            indices(0, 0)
            for k in range(FS):
                gather(0, k, P, 0)

            def group_of(t, half):
                indices(t + FS, half)
                for k in range(FS):
                    gather(t + FS, k, P, half)
                    rstd_of(t, k, P)

            LATER = FLOOP // FS - 2
            group_of(0, 1)
            with pool.Fori(0, LATER // 2) as group:
                for half in range(2):
                    group_of((group * 2 + half + 1) * FS, half)
            assert LATER % 2 == 1
            group_of(LATER * FS, 0)
            indices(FLOOP, 1)
            for k in range(FS):
                if FLOOP + k <= FULL:
                    gather(FLOOP, k, P if FLOOP + k < FULL else TAIL, 1)
                rstd_of(FLOOP - FS, k, P)
            for k in range(FULL - FLOOP + 1):
                rstd_of(FLOOP, k, P if FLOOP + k < FULL else TAIL)

        @block.vector
        def _(dve):
            v = nc.vector
            for s in (tg_cp, w_ok, b_ok, mv_ok, t_ok, u_ok, edge_ok, st_ok, f_sum, f_st, f_mv, f_o):
                dve.sem_inc(s, PRIME)
            steps = [0]

            def link(ins, *also):
                steps[0] += 1
                ins.then_inc(v_step, 1)
                dve.wait_ge(v_step, steps[0])

            link(v.memset(zero_bf, 0.0))
            link(v.memset(ones2[:, :].bitcast(f32), 1.0))
            link(v.memset(ntab, 0.0))
            link(v.memset(q0b, 0.0))
            link(v.memset(zcol[:, :], 0.0))
            dve.wait_ge(h_st[0], 16)
            dve.wait_ge(h_st[1], 16)
            for n, e in enumerate((src_i, dst_i)):
                link(v.tensor_scalar(hilo_i[:, 2 * n, :], e, 7, None, ALU.logical_shift_right))
                link(v.tensor_scalar(hilo_i[:, 2 * n + 1, :], e, P - 1, None, ALU.bitwise_and))
            link(v.tensor_copy(hilo, hilo_i))
            link(v.memset(idx_now[:, NE:], 0.0))
            link(v.memset(idx_h[:, NE:], 0.0))
            link(v.memset(idx_l[:, NE:], 0.0))
            link(v.memset(em, 0.0))
            link(v.tensor_scalar(pay[:, :, 3], src_i, float(N - 1), None, ALU.min))
            dve.wait_ge(p_step, 13)
            link(v.tensor_copy(iota[:, :], iota_i))
            link(v.tensor_copy(iota_b, iota_i))
            for n, h in enumerate(hot):
                w = h.shape[2]
                v.tensor_tensor(h, iota_b[:, 0:w].unsqueeze(1).to_broadcast([P, NE, w]),
                                hilo[:, n, :].unsqueeze(2).to_broadcast([P, NE, w]), ALU.is_equal)\
                 .then_inc(hot_ok, 1)
            link(v.tensor_scalar(valid, node_i, float(N), None, ALU.is_lt))
            dve.wait_ge(hist_ok, 2)
            link(v.tensor_copy(outs, ps_s[0][0:NR, 0:P]))
            link(v.tensor_copy(ins, ps_s[1][0:NR, 0:P]))
            v.tensor_scalar(t1, outs, 1.0, None, ALU.max).then_inc(deg_ok, 1)
            v.tensor_scalar(t2, ins, 1.0, None, ALU.max).then_inc(deg_ok, 1)
            link(v.scalar_tensor_tensor(act_l, ins, 0.0, valid, ALU.is_gt, ALU.mult))
            link(v.scalar_tensor_tensor(act_m, outs, 0.0, act_l, ALU.is_gt, ALU.mult))
            link(v.tensor_tensor_scan(scan_l, ones_np, act_l, 0.0, ALU.mult, ALU.add))
            link(v.tensor_tensor_scan(scan_m, ones_np, act_m, 0.0, ALU.mult, ALU.add))
            v.tensor_copy(row_sums[:, 0:1], scan_l[:, P - 1:P]).then_inc(sums_ok, 1)
            v.tensor_copy(row_sums[:, 1:2], scan_m[:, P - 1:P]).then_inc(sums_ok, 1)
            dve.wait_ge(pre_ok, 2)
            link(v.tensor_copy(before, ps_s[0][0:NR, 0:2]))
            link(v.tensor_copy(totals, ps_s[1][:, 0:2]))
            c_last, c_mid = ntab[:, :, C_LAST], ntab[:, :, C_MID]
            link(v.scalar_tensor_tensor(c_last, scan_l, before[:, 0:1], act_l, ALU.add, ALU.subtract))
            link(v.scalar_tensor_tensor(c_mid, scan_m, before[:, 1:2], act_m, ALU.add, ALU.subtract))
            link(v.scalar_tensor_tensor(t3, c_mid, totals[0:NR, 1:2], act_l, ALU.subtract, ALU.mult))
            link(v.tensor_scalar(ntab[:, :, C_ROW], t3, totals[0:NR, 1:2], None, ALU.add))
            link(v.scalar_tensor_tensor(t3, c_last, totals[0:NR, 0:1], act_l, ALU.subtract, ALU.mult))
            v.tensor_scalar(fidx, t3, totals[0:NR, 0:1], None, ALU.add).then_inc(fid_ok, 1)
            dve.wait_ge(pow_ok, 2)
            for deg, root in ((t1, r1), (t2, r2)):
                link(v.reciprocal(root, root))
                link(v.tensor_tensor(deg, deg, root, ALU.mult))
                link(v.tensor_tensor(deg, deg, root, ALU.mult))
                link(v.tensor_scalar(deg, deg, -0.5, 1.5, ALU.mult, ALU.add))
            link(v.tensor_tensor(ntab[:, :, C_NOUT], t1, r1, ALU.mult))
            link(v.tensor_tensor(t2, t2, r2, ALU.mult))
            link(v.tensor_tensor(ntab[:, :, C_NIN], t2, valid, ALU.mult))
            link(v.tensor_tensor(ntab[:, :, C_NINM], t2, act_m, ALU.mult))
            v.engine_nop().then_inc(table_ok, 1)
            link(v.tensor_scalar(cnt_f, totals[0:1, :], float(2 * P), None, ALU.add))
            link(v.tensor_copy(cnt_i, cnt_f))
            link(v.tensor_scalar(cnt_i2, cnt_i, 8, None, ALU.logical_shift_right))
            link(v.tensor_scalar(counts[0:1, 0:1], cnt_i2[:, 1:2], 3.0, -3.0, ALU.max, ALU.add))
            link(v.tensor_scalar(counts[0:1, 1:2], cnt_i2[:, 0:1], 3.0, -3.0, ALU.max, ALU.add))
            dve.wait_ge(fidt_ok, 1)
            link(v.tensor_copy(idx_f[:, :], ps_s[0][:, 0:NR]))
            with dve.Fori(0, NE // FS) as group:
                i = group * FS
                for k in range(FS):
                    for got, one, kept in ((tg_d, dslot, dtab), (tg_s, sslot, stab)):
                        dve.wait_ge(got[k], i * 4 + 16)
                        dve.sem_inc(dve_tick, 1)
                        v.tensor_copy(kept[:, bass.ds(i + k, 1), :], one[:, k:k + 1, :]).then_inc(tg_cp, 1)
            dve.wait_ge(tg_cp, done(2 * NE))
            link(v.tensor_tensor(wgt_l[:, 0:NE], dtab[:, :, C_NIN], stab[:, :, C_NOUT], ALU.mult))
            link(v.tensor_tensor(pay[:, :, 1], dtab[:, :, C_NINM], stab[:, :, C_NOUT], ALU.mult))
            link(v.tensor_copy(pay[:, :, 0], stab[:, :, C_ROW]))
            link(v.tensor_copy(idx_l[:, 0:NE], stab[:, :, C_ROW]))
            for pad in (wgt_m, wgt_l, rel_m, rel_l):
                link(v.memset(pad[:, NE:NE + 2], 0.0))
            v.tensor_scalar(keep, dtab[:, :, C_NINM], 0.0, None, ALU.is_gt).then_inc(keep_ok, 1)
            link(v.tensor_copy(other, edge_i))
            dve.wait_ge(place_ok, 2)
            link(v.tensor_copy(col_sum, ps_s[3][:, 0:NE]))
            link(v.tensor_tensor_scan(col_scan, ones[:, 0:NE], col_sum, 0.0, ALU.mult, ALU.add))
            needed = col_scan[:, NE - 1:NE]
            link(v.tensor_tensor(pos, col_scan, col_sum, ALU.subtract))
            link(v.tensor_tensor(pos, ps_s[2][:, 0:NE], pos, ALU.add))
            link(v.scalar_tensor_tensor(other, other, needed, pos, ALU.add, ALU.subtract))
            link(v.tensor_tensor(pos, pos, other, ALU.subtract))
            link(v.tensor_tensor(pos, pos, keep, ALU.mult))
            link(v.tensor_tensor(target, pos, other, ALU.add))
            link(v.scalar_tensor_tensor(pos, dtab[:, :, C_MID], totals[:, 1:2], keep, ALU.subtract, ALU.mult))
            link(v.tensor_scalar(pay[:, :, 2], pos, totals[:, 1:2], None, ALU.add))
            link(v.tensor_scalar(limits, iota[0:1, 0:NE // UN], float(UN * ET), needed[0:1, :], ALU.mult, ALU.is_lt))
            link(v.tensor_reduce(its_f, limits, mybir.AxisListType.X, ALU.add))
            link(v.tensor_scalar(counts[0:1, 2:3], its_f, 4.0, -4.0, ALU.max, ALU.add))

            def edges_out(i, half):
                own = slice(half * FS, half * FS + FS)
                v.tensor_copy(slot2[:, own], target[:, bass.ds(i + half * FS, FS)]).then_inc(pay_ok, 1)
                v.tensor_copy(pay_slot[:, own, :], pay[:, bass.ds(i + half * FS, FS), :]).then_inc(pay_ok, 1)

            for half in range(2):
                edges_out(0, half)
            with dve.Fori(1, NE // (2 * FS)) as group:
                for half in range(2):
                    dve.wait_ge(sc_st[half], group * (FS * 16))
                    dve.sem_inc(dve_tick, 1)
                    edges_out(group * (2 * FS), half)
            dve.wait_ge(em_in, 16)
            v.engine_nop().then_inc(keep_ok, 1)
            link(v.tensor_copy(wgt_m[:, 0:NE], em[:, :, 1]))
            link(v.tensor_copy(idx_h[:, 0:NE], em[:, :, 0]))
            link(v.tensor_copy(idx_now[:, 0:NE], em[:, :, 3]))
            dve.wait_ge(pick_ok, 2)
            for n, (c, rel, q0) in enumerate(((em[:, :, 2], rel_m, q0_m), (dtab[:, :, C_LAST], rel_l, q0_l))):
                link(v.tensor_copy(q0b[:, n, 1:NE], ps_s[n][:, 0:NE - 1]))
                link(v.tensor_tensor(rel[:, 0:NE], c, q0b[:, n, :], ALU.subtract))
                link(v.tensor_copy(q0[:, :], q0b[0:1, n, :]))
            v.engine_nop().then_inc(setup_ok, 1)
            pairs_m, pairs_l, nbm, nbl, its_m, nem = tile_counts(dve)

            SB = NE + 2

            def select(L, i, k, rel, wgt):
                v.tensor_scalar(sel[:, k % 2, :], iota[:, :], rel[:, bass.ds(i, 1)], wgt[:, bass.ds(i, 1)],
                                ALU.is_equal, ALU.mult).then_inc(sel_ok, 1)

            def indices(t, half):
                v.tensor_copy(slot[:, half * GS:half * GS + GS], idx_now[:, bass.ds(t, GS)]).then_inc(ix_ok, 1)

            def zero_tail(nb):
                v.tensor_copy(agg_t[:, :, bass.ds((nb - 2) * P, 2 * P)],
                              zcol[:, :].unsqueeze(2).to_broadcast([P, KB, 2 * P])).then_inc(v_tail, 1)

            def sum_stage(L, rel, wgt, q0, its):
                base = L * nbm
                dve.wait_ge(lo_ok, done(base))
                dve.sem_inc(dve_tick, 1)
                v.memset(agg_t[:, :, 0:1], 0.0).then_inc(zero_ok, 1)
                indices(0, 0)
                for k in range(2):
                    select(L, k, k, rel, wgt)
                def tiles(first, end):
                    with dve.Fori(first, end) as group:
                        t = group * UN
                        i = L * nem + t
                        for k in range(UN):
                            r0 = dve.value_load(q0[0:1, bass.ds(t + k, 1)], min_val=0, max_val=N)
                            dve.wait_ge(agg_ok, done(i + k + 1))
                            select(L, t + k + 2, k, rel, wgt)
                            dve.wait_ge(edge_ok, done(i + k))
                            dve.sem_inc(dve_tick, 1)
                            dve.wait_ge(ev_ok, done(i + k + 1))
                            col = agg_t[:, :, bass.ds(r0, 1)]
                            v.tensor_tensor(col, ps_a[k % GS][:, :, 0:1], col, ALU.add).then_inc(edge_ok, 1)
                            if k % GS == 0:
                                indices(t + k + GS, 1 - k // GS)

                for q in range(KB):
                    if q % 2 == 0:
                        tiles(q // 2, q // 2 + 1)
                    if q == 0:
                        dve.wait_ge(y_ok, done(base))
                        dve.sem_inc(dve_tick, 1)
                    dve.wait_ge(raw_in[q % 2], (L * 2 + q // 2 + 1) * 16)
                    dve.sem_inc(dve_tick, 1)
                    v.tensor_copy(w_hi[:, q, :], w_raw[:, q % 2, :]).then_inc(wh_ok, 1)
                    dve.wait_ge(wh_ok, L * KB + q + 1)
                    v.tensor_tensor(w_lo[:, q, :], w_raw[:, q % 2, :], w_hi[:, q, :].bitcast(f32), ALU.subtract)\
                     .then_inc(w_ok, 1)
                tiles(2, 3)
                dve.wait_ge(b_in, (L + 1) * 16)
                dve.sem_inc(dve_tick, 1)
                v.tensor_copy(b_high, b_raw[0:2, 0, :]).then_inc(bh_ok, 1)
                dve.wait_ge(bh_ok, L + 1)
                v.scalar_tensor_tensor(b_rows[:, :], b_high.bitcast(f32), negm[:, :], b_raw[0:2, 0, :],
                                       ALU.mult, ALU.add).then_inc(b_ok, 1)
                tiles(3, its)
                v.tensor_copy(idx_now[:, :], idx_h[:, :]).then_inc(now_ok, 1)

            def centre(j, k):
                dve.wait_ge(y_ok, done(j + 1))
                v.bn_stats(stats[:, k, :], ps_y[k][:, :]).then_inc(st_ok, 1)
                dve.wait_ge(st_ok, done(j + 1))
                dve.sem_inc(dve_tick, 1)
                v.bn_aggr(mv[:, k, :], stats[:, k, :]).then_inc(mv_ok, 1)
                dve.wait_ge(h_ok, done(j - 1))
                dve.wait_ge(mv_ok, done(j + 1))
                dve.sem_inc(dve_tick, 1)
                v.scalar_tensor_tensor(rows[:, k, :], ps_y[k][:, :], mv[:, k, 0:1], gam,
                                       ALU.subtract, ALU.mult).then_inc(t_ok, 1)

            def scale(j, k):
                dve.wait_ge(t_ok, done(j + 1))
                dve.sem_inc(dve_tick, 1)
                dve.wait_ge(rs_ok, done(j + 1))
                v.scalar_tensor_tensor(rows[:, k, :], rows[:, k, :], rstd[:, k:k + 1], bet[:, :],
                                       ALU.mult, ALU.add).then_inc(u_ok, 1)

            def w_stage(L, pairs):
                base, nb = L * nbm, pairs * 2
                dve.wait_ge(gb_in, (L + 1) * 32)
                dve.sem_inc(dve_tick, 1)
                centre(base, 0)
                with dve.Fori(0, pairs - 1) as pair:
                    j = base + pair * 2
                    for k in range(2):
                        centre(j + k + 1, 1 - k)
                        scale(j + k, k)
                centre(base + nb - 1, 1)
                scale(base + nb - 2, 0)
                scale(base + nb - 1, 1)

            link(v.memset(agg_t[:, :, 1:4 * P], 0.0))
            zero_tail(nbm)
            with dve.Fori(0, LAYERS - 1) as L:
                sum_stage(L, rel_m, wgt_m, q0_m, its_m)
                w_stage(L, pairs_m)
            dve.wait_ge(lo_ok, done((LAYERS - 1) * nbm))
            dve.sem_inc(dve_tick, 1)
            zero_tail(nbl)
            v.tensor_copy(idx_now[:, :], idx_l[:, :]).then_inc(now_ok, 1)
            dve.wait_ge(now_ok, LAYERS)
            sum_stage(LAYERS - 1, rel_l, wgt_l, q0_l, NE // UN)
            w_stage(LAYERS - 1, pairs_l)

            def width(n):
                return P if n < FULL else TAIL

            def step(t, k, first=False):
                end = isinstance(t, int)
                if not end or t + k + 2 <= FULL:
                    t2, k2 = t + (k + 2) // FS * FS, (k + 2) % FS
                    n2 = width(t + k + 2) if end else P
                    add(t2, k2, n2)
                if not end or t + k + 1 <= FULL:
                    mean(t + (k + 1) // FS * FS, (k + 1) % FS, width(t + k + 1) if end else P)
                if not end or t + k + 2 <= FULL:
                    spread(t2, k2, n2)
                result(t, k, width(t + k) if end else P, first)

            def add(t, k, n):
                for arrived in (xf_in, hf_in):
                    dve.wait_ge(arrived[k], t * (16 // FS) + 16)
                    dve.sem_inc(dve_tick, 1)
                v.tensor_tensor(xs[0:n, k, :], xs[0:n, k, :], hf[0:n, k, :], ALU.add).then_inc(f_sum, 1)

            def spread(t, k, n):
                dve.wait_ge(f_sum, done(t + k + 1))
                v.bn_stats(stats[0:n, k, :], xs[0:n, k, :]).then_inc(f_st, 1)

            def mean(t, k, n):
                dve.wait_ge(f_st, done(t + k + 1))
                dve.sem_inc(dve_tick, 1)
                v.bn_aggr(mv[0:n, k, :], stats[0:n, k, :]).then_inc(f_mv, 1)

            def result(t, k, n, first):
                dve.wait_ge(f_mv, done(t + k + 1))
                dve.sem_inc(dve_tick, 1)
                dve.wait_ge(f_rs, done(t + k + 1))
                dve.sem_inc(dve_tick, 1)
                if not first:
                    dve.wait_ge(o_st[k], t * (16 // FS))
                    dve.sem_inc(dve_tick, 1)
                v.tensor_scalar(of[0:n, k, :], xs[0:n, k, :], mv[0:n, k, 0:1], rstd[0:n, k:k + 1],
                                ALU.subtract, ALU.mult).then_inc(f_o, 1)

            for k in range(2):
                add(0, k, P)
                spread(0, k, P)
            mean(0, 0, P)
            for k in range(FS):
                step(0, k, first=True)
            with dve.Fori(1, FLOOP // FS - 1) as group:
                for k in range(FS):
                    step(group * FS, k)
            for n in range(FLOOP - FS, FULL + 1):
                step(n - n % FS, n % FS)

        @block.scalar
        def _(act):
            a = nc.scalar
            for s in (ev_ok, hi_ok, h_ok):
                act.sem_inc(s, PRIME)
            act.wait_ge(deg_ok, 2)
            a.activation(r1, t1, ACT.Sqrt).then_inc(pow_ok, 1)
            a.activation(r2, t2, ACT.Sqrt).then_inc(pow_ok, 1)
            act.preload_act_table(ACT.Gelu)
            pairs_m, pairs_l, nbm, nbl, its_m, nem = tile_counts(act)

            def hold(s, n):
                act.wait_ge(s, n)
                act.sem_inc(act_tick, 1)

            def sum_stage(L, q0, its):
                hold(lo_ok, done(L * nbm))
                with act.Fori(0, its) as group:
                    t = group * UN
                    for k in range(UN):
                        i = L * nem + t
                        r0 = act.value_load(q0[0:1, bass.ds(t + k, 1)], min_val=0, max_val=N)
                        hold(agg_ok, done(i + k + 1))
                        hold(ev_ok, done(i + k))
                        a.activation(agg_t[:, :, bass.ds(r0 + 1, P - 1)], ps_a[k % GS][:, :, 1:P], ACT.Copy)\
                         .then_inc(ev_ok, 1)

            def high(j, c, k):
                hold(y_ok, done(j - 1))
                a.activation(s_hi[:, k, :, :], agg_t[:, :, bass.ds(c * P, P)], ACT.Copy).then_inc(hi_ok, 1)

            def gelu(j, j_pair, k):
                hold(u_ok, done(j + 1))
                hold(h_st[k], j_pair * 8 + 16)
                a.activation(rows[:, 2 + k, :], rows[:, k, :], ACT.Gelu).then_inc(h_ok, 1)

            def w_stage(L, pairs, ne):
                base, nb = L * nbm, pairs * 2
                hold(edge_ok, done(L * nem + ne))
                hold(ev_ok, done(L * nem + ne))
                hold(b_ok, done(L + 1))
                for n in range(3):
                    high(base + n, n, n % 2)
                with act.Fori(0, pairs - 2) as pair:
                    c = pair * 2
                    for k in range(2):
                        j = base + c
                        high(j + k + 3, c + k + 3, 1 - k)
                        gelu(j + k, j, k)
                high(base + nb - 1, nb - 1, 1)
                for n in range(4, 0, -1):
                    gelu(base + nb - n, base + nb - n - n % 2, n % 2)

            with act.Fori(0, LAYERS - 1) as L:
                sum_stage(L, q0_m, its_m)
                w_stage(L, pairs_m, nem)
            sum_stage(LAYERS - 1, q0_l, NE // UN)
            w_stage(LAYERS - 1, pairs_l, NE)

            act.sem_inc(f_ve, PRIME)

            def add_eps(t, k, n):
                hold(f_mv, done(t + k + 1))
                a.activation(var[0:n, k:k + 1], mv[0:n, k, 1:2], ACT.Copy, bias=EPS).then_inc(f_ve, 1)

            with act.Fori(0, FLOOP // FS) as group:
                for k in range(FS):
                    add_eps(group * FS, k, P)
            for k in range(FULL - FLOOP + 1):
                add_eps(FLOOP, k, P if FLOOP + k < FULL else TAIL)

        @block.tensor
        def _(pe):
            mm = nc.tensor.matmul
            for s in (agg_ok, y_ok):
                pe.sem_inc(s, PRIME)
            for n in range(2):
                pe.wait_ge(hot_ok, 2 * n + 2)
                acc = ps_s[n][0:NR, 0:P]
                mm(acc, zero_bf[:, 0:NR], zero_bf, start=True, stop=False)
                with pe.Fori(0, NE // 16) as group:
                    for k in range(16):
                        i = group * 16 + k
                        mm(acc, hot[2 * n][:, bass.ds(i, 1), :].rearrange("p a b -> p (a b)"),
                           hot[2 * n + 1][:, bass.ds(i, 1), :].rearrange("p a b -> p (a b)"),
                           start=False, stop=False)
                mm(acc, zero_bf[:, 0:NR], zero_bf, start=False, stop=True).then_inc(hist_ok, 1)
            pe.wait_ge(sums_ok, 2)
            mm(ps_s[0][0:NR, 0:2], lower, row_sums, start=True, stop=True).then_inc(pre_ok, 1)
            mm(ps_s[1][:, 0:2], ones_np, row_sums, start=True, stop=True).then_inc(pre_ok, 1)
            pe.wait_ge(fid_ok, 1)
            nc.tensor.transpose(ps_s[0][:, 0:NR], fidx, ident[0:NR, 0:NR]).then_inc(fidt_ok, 1)
            pe.wait_ge(keep_ok, 1)
            mm(ps_s[2][:, 0:NE], before_p, keep, start=True, stop=True).then_inc(place_ok, 1)
            mm(ps_s[3][:, 0:NE], ones, keep, start=True, stop=True).then_inc(place_ok, 1)
            pe.wait_ge(keep_ok, 2)
            mm(ps_s[0][:, 0:NE], pick, em[:, :, 2], start=True, stop=True).then_inc(pick_ok, 1)
            mm(ps_s[1][:, 0:NE], pick, dtab[:, :, C_LAST], start=True, stop=True).then_inc(pick_ok, 1)
            pairs_m, pairs_l, nbm, nbl, its_m, nem = tile_counts(pe)

            def sum_stage(L, its):
                with pe.Fori(0, its) as group:
                    for k in range(UN):
                        i = L * nem + group * UN
                        pe.wait_ge(g_in[k % GS], (L * (its_m * 2) + group * 2 + k // GS + 1) * 16)
                        pe.sem_inc(pe_tick, 1)
                        pe.wait_ge(sel_ok, i + L * 2 + k + 1)
                        pe.sem_inc(pe_tick, 1)
                        pe.wait_ge(ev_ok, done(i + k - GS + 1))
                        pe.wait_ge(edge_ok, done(i + k - GS + 1))
                        pe.sem_inc(pe_tick, 1)
                        for b in range(KB):
                            m = mm(ps_a[k % GS][:, b, :], rows[:, k % GS, b * P:(b + 1) * P], sel[:, k % 2, :],
                                   start=True, stop=True)
                        m.then_inc(agg_ok, 1)

            def w_stage(L, pairs):
                base, nb = L * nbm, pairs * 2
                pe.wait_ge(w_ok, done(L * KB + KB))
                pe.sem_inc(pe_tick, 1)
                pe.wait_ge(b_ok, done(L + 1))
                pe.sem_inc(pe_tick, 1)
                with pe.Fori(0, pairs) as pair:
                    c = pair * 2
                    for k in range(2):
                        j = base + c
                        pe.wait_ge(lo_ok, done(j + k + 1))
                        pe.sem_inc(pe_tick, 1)
                        pe.wait_ge(t_ok, done(j + k - 1))
                        pe.sem_inc(pe_tick, 1)
                        mm(ps_y[k][:, :], ones2[:, :], b_rows[:, :], start=True, stop=False)
                        for b in range(KB):
                            for s, w in ((s_hi, w_hi), (s_hi, w_lo), (s_lo, w_hi)):
                                last = s is s_lo and b == KB - 1
                                m = mm(ps_y[k][:, :], s[:, k, b, :], w[:, b, :], start=False, stop=last)
                        m.then_inc(y_ok, 1)

            with pe.Fori(0, LAYERS - 1) as L:
                sum_stage(L, its_m)
                w_stage(L, pairs_m)
            sum_stage(LAYERS - 1, NE // UN)
            w_stage(LAYERS - 1, pairs_l)


def kernel(x, src, dst, L0_gnn_Ws, L0_gnn_bs, L0_gnn_ln_g, L0_gnn_ln_b):
    import numpy as np
    import concourse.bacc as bacc
    from concourse.bass_utils import run_bass_kernel_spmd as run

    def tiles(e):
        flat = np.full(NE * ET, N, e.dtype)
        flat[:E] = e
        laid = np.full((P, NE), N, e.dtype)
        laid[:ET] = flat.reshape(NE, ET).T
        return laid

    arrays = {"in_x": np.ascontiguousarray(x), "in_src": tiles(np.asarray(src)), "in_dst": tiles(np.asarray(dst)),
              "in_Ws": np.ascontiguousarray(L0_gnn_Ws), "in_bs": np.ascontiguousarray(L0_gnn_bs),
              "in_ln_g": np.ascontiguousarray(L0_gnn_ln_g), "in_ln_b": np.ascontiguousarray(L0_gnn_ln_b)}
    nc = bacc.Bacc("TRN2", target_bir_lowering=False, num_devices=1)
    args = [nc.dram_tensor(k, v.shape, mybir.dt.from_np(v.dtype), kind="ExternalInput").ap()
            for k, v in arrays.items()]
    args.append(nc.dram_tensor("out_0", (N, D), f32, kind="ExternalOutput").ap())
    build(nc, *args)
    return run(nc, [arrays], core_ids=[0]).results[0]["out_0"]
```

```python
import concourse.bass as bass
from concourse import mybir
from contextlib import ExitStack

N = 10000
E = 10000
D = 512
LAYERS = 8
EPS = 1e-5
P = 128
KB = D // P
ET = P - 1
NE = 80
NR = 80
PADDED = NR * P
GS = 5
UN = 2 * GS
ES = 4
FS = 8
COLS = 8
TS = 8
C_ROW, C_NIN, C_NOUT = range(3)
LEVELS = 3
SETS = LEVELS + 2
ITS_MIN, PAIRS_MIN = 3, 3
PRIME = 8

f32, f32r, i32, bf16 = mybir.dt.float32, mybir.dt.float32r, mybir.dt.int32, mybir.dt.bfloat16
ALU = mybir.AluOpType
ACT = mybir.ActivationFunctionType


def done(n):
    return n + PRIME


def build(nc, x, src, dst, dst_prev, dst_row, Ws, bs, ln_g, ln_b, out):
    hbuf = nc.dram_tensor("h_rows", (PADDED, D), f32).ap()
    ntab_d = nc.dram_tensor("node_table", (PADDED, COLS), f32).ap()
    ranks_d = nc.dram_tensor("node_table_with_ranks", (PADDED, COLS), f32).ap()
    edges_d = nc.dram_tensor("edges_by_rank", (NE * ET, 4), f32).ap()
    ctx = ExitStack()
    with ctx:
        def sb(n, s, d=f32):
            return ctx.enter_context(nc.sbuf_tensor(n, s, d))

        def sem(n):
            return ctx.enter_context(nc.semaphore(n))

        agg_t = sb("agg_t", [P, KB, PADDED])
        w_hi = sb("w_hi", [P, KB, D], f32r)
        w_lo = sb("w_lo", [P, KB, D], f32r)
        w_raw = sb("w_raw", [P, 2, D])
        b_rows = sb("b_rows", [2, D], f32r)
        zcol = sb("zcol", [P, KB])
        b_raw = w_raw
        bet = sb("bet", [P, D])
        s_hi = sb("s_hi", [P, 2, KB, P], f32r)
        s_lo = sb("s_lo", [P, 2, KB, P], f32r)
        b_high = s_hi[0:2, 0, :, :].rearrange("p a b -> p (a b)")
        rows = sb("rows", [P, GS, D])
        gam = rows[:, 4, :]
        sel = sb("sel", [P, 2, P])
        iota = sb("iota", [P, P])
        ones2 = sb("ones2", [2, P], f32r)
        negm = sb("negm", [2, 1])
        idx_now = sb("idx_now", [P, NE + GS], i32)
        idx_h = sb("idx_h", [P, NE + GS], i32)
        idx_f = sb("idx_f", [P, NR], i32)
        wgt = sb("wgt", [P, NE + 2])
        rel = sb("rel", [P, NE + 2])
        q0 = sb("q0", [1, NE], i32)
        pairs_t = sb("pairs_t", [1, LAYERS], i32)
        its_t = sb("its_t", [1, LAYERS], i32)
        base_p = sb("base_p", [1, LAYERS], i32)
        base_i = sb("base_i", [1, LAYERS], i32)
        slot = sb("slot", [P, UN], i32)
        slot2 = sb("slot2", [P, 2 * FS], i32)
        stats = sb("stats", [P, FS, 6])
        mv = sb("mv", [P, FS, 2])
        var = sb("var", [P, FS])
        rstd = sb("rstd", [P, FS])
        mhalf = sb("mhalf", [P, 1])

        ps_a = [ctx.enter_context(nc.psum_tensor(f"ps_a{i}", [P, KB, P], f32)) for i in range(GS)]
        ps_y = [ctx.enter_context(nc.psum_tensor(f"ps_y{i}", [P, D], f32)) for i in range(2)]
        ps_s = [ps_a[i][:, :, :].rearrange("p k n -> p (k n)") for i in range(4)]

        class Space:
            at = 0

        def part(shape, d=f32):
            size = 1
            for v in shape[1:]:
                size *= v
            words = size * (2 if d is bf16 else 4) // 4
            flat = agg_t[:, :, :].rearrange("p k n -> p (k n)")[0:shape[0], Space.at:Space.at + words]
            Space.at += words
            if d is not f32:
                flat = flat.bitcast(d)
            if len(shape) == 3:
                flat = flat.rearrange("p (a b) -> p a b", b=shape[2])
            return flat

        src_i = part([P, NE], i32)
        dst_i = part([P, NE], i32)
        prev_i = part([P, NE], i32)
        hilo_i = part([P, 4, NE], i32)
        hilo = part([P, 4, NE], bf16)
        iota_b = part([P, P], bf16)
        hot = [part([P, NE, n], bf16) for n in (NR, P, NR, P)]
        zero_bf = part([P, P], bf16)
        zero_row = part([P, D])
        node_i = part([NR, P], i32)
        rows_i = part([NR, 1], i32)
        iota_i = part([P, P], i32)
        valid = part([NR, P])
        outs, ins = part([NR, P]), part([NR, P])
        sets = part([NR, SETS, P])
        only = part([NR, SETS, P])
        scans = part([NR, SETS, P])
        row_sums = part([NR, SETS])
        before = part([NR, SETS])
        totals, reach = part([P, SETS]), part([P, SETS])
        flags_b = part([NR, P], bf16)
        spot = Space.at
        dst_hi = part([NR, NE * P], i32)
        after, Space.at = Space.at, spot
        picked = part([P, NE, P], bf16)
        keep, fresh, col_sum, col_scan, pos = [part([P, SETS + 1, NE]) for _ in range(5)]
        is_new, sets_of = part([P, NE]), part([P, NE])
        place, past = part([P, NE]), part([P, NE])
        target = part([P, NE], i32)
        assert Space.at <= after
        Space.at = after
        at_hi = part([NR, NE * P], bf16)
        row_no = part([NR, 1])
        flag_e = part([P, NE])
        hot_f = hot[2]
        ones = part([P, P])
        all_ones = part([P, (SETS + 1) * NE])
        ones_np = ones[0:NR, :]
        before_p = part([P, P])
        lower = before_p[0:NR, 0:NR]
        ntab = part([NR, P, COLS])
        t1, t2 = part([NR, P]), part([NR, P])
        r1, r2 = part([NR, P]), part([NR, P])
        fidx = part([NR, P])
        ident = part([P, P])
        pick = part([P, P])
        dtab = part([P, NE, COLS])
        stab = part([P, NE, COLS])
        tslot = part([P, TS, COLS])
        q0b = part([P, NE])
        pay = part([P, NE, 4])
        em = part([P, NE, 4])
        pay_slot = part([P, 2 * ES, 4])
        limits = part([1, SETS, NE // UN])
        ends = part([1, SETS])
        its_f = part([1, SETS])
        cnt_f, cnt_i = part([1, SETS]), part([1, SETS], i32)
        lay_f = part([1, 4, LAYERS])
        assert Space.at <= KB * PADDED, Space.at
        Space.at = 0
        xs = part([P, FS, D])
        hf = part([P, FS, D])
        of = part([P, FS, D])

        hot_ok = sem("one_hots_made")
        hist_ok = sem("histograms_done")
        deg_ok = sem("degrees_clipped")
        pow_ok = sem("norms_made")
        sums_ok = sem("row_sums_made")
        pre_ok = sem("prefix_done")
        flags_ok = sem("node_flags_made")
        gath_ok = sem("flags_of_rows_out")
        pick_f = sem("flags_picked")
        fl_ok = sem("flagged_one_hots_made")
        lev_ok = sem("level_done")
        row_in = sem("dst_rows_in")
        fid_ok = sem("final_index_made")
        fidt_ok = sem("final_index_transposed")
        table_ok = sem("node_table_made")
        pick_ok = sem("first_ranks_spread")
        keep_ok = sem("edge_sets_marked")
        place_ok = sem("places_summed")
        pay_ok = sem("edges_in_slots")
        sc_st = [sem(f"edges_scattered{k}") for k in range(2)]
        em_in = sem("edges_by_rank_in")
        v_step = sem("vector_steps")
        p_step = sem("pool_setup_steps")
        rows_clear = sem("zero_row_made")
        h_clear = sem("h_cleared")
        nt_st = sem("node_table_stored")
        rk_st = sem("ranks_stored")
        prev_in = sem("dst_prev_in")
        tick = sem("pool_ticks")
        cp_idx = sem("index_copied")
        tg_in = [sem(f"table_row_in{k}") for k in range(TS)]
        tg_cp = sem("table_rows_kept")
        setup_ok = sem("setup_done")
        g_in = [sem(f"rows_gathered{k}") for k in range(GS)]
        sel_ok = sem("selection_made")
        ix_ok = sem("gather_indices_ready")
        now_ok = sem("indices_switched")
        agg_ok = sem("tile_summed")
        ev_ok = sem("sums_kept")
        edge_ok = sem("first_column_added")
        raw_in = [sem(f"w_chunk_in{k}") for k in range(2)]
        b_in = sem("bias_in")
        gb_in = sem("gamma_beta_in")
        w_ok = sem("w_chunk_split")
        b_ok = sem("bias_split")
        hi_ok = sem("high_half_made")
        lo_ok = sem("low_half_made")
        y_ok = sem("product_done")
        st_ok = sem("stats_made")
        act_tick = sem("act_ticks")
        dve_tick = sem("dve_ticks")
        mv_ok = sem("mean_var_made")
        var_ok = sem("var_eps_made")
        rs_ok = sem("rstd_made")
        t_ok = sem("centred")
        u_ok = sem("normalised")
        h_ok = sem("gelu_done")
        h_st = [sem(f"h_stored{k}") for k in range(2)]
        pe_tick = sem("pe_ticks")
        sp_tick = sem("sp_ticks")
        wh_ok = sem("w_high_made")
        bh_ok = sem("bias_high_made")
        v_tail = sem("tail_cleared")
        zero_ok = sem("column_cleared")
        xf_in = [sem(f"x_tile_in{k}") for k in range(FS)]
        hf_in = [sem(f"h_tile_in{k}") for k in range(FS)]
        f_sum = sem("residual_added")
        f_st = sem("final_stats")
        f_mv = sem("final_mean_var")
        f_ve = sem("final_var_eps")
        f_rs = sem("final_rstd")
        f_o = sem("final_rows_made")
        o_st = [sem(f"out_stored{k}") for k in range(FS)]
        o_last = sem("out_tail_stored")

        block = ctx.enter_context(nc.Block())

        def layer_counts(eng, L):
            own = bass.ds(L, 1)
            pairs = eng.value_load(pairs_t[0:1, own], min_val=0, max_val=NR // 2 - PAIRS_MIN) + PAIRS_MIN
            its = eng.value_load(its_t[0:1, own], min_val=0, max_val=NE // UN - ITS_MIN) + ITS_MIN
            pb = eng.value_load(base_p[0:1, own], min_val=0, max_val=LAYERS * NR // 2)
            ib = eng.value_load(base_i[0:1, own], min_val=0, max_val=LAYERS * NE // UN)
            return pairs, its, pb, ib

        def all_tiles(eng):
            last = LAYERS - 1
            pairs = eng.value_load(pairs_t[0:1, last:last + 1], min_val=0, max_val=NR // 2 - PAIRS_MIN) + PAIRS_MIN
            pb = eng.value_load(base_p[0:1, last:last + 1], min_val=0, max_val=LAYERS * NR // 2)
            return pb * 2 + pairs * 2

        FULL = N // P
        TAIL = N - FULL * P
        FLOOP = FULL // FS * FS

        @block.sync
        def _(sp):
            sp.dma_start(src_i, src).then_inc(h_st[0], 16)
            sp.dma_start(dst_i, dst).then_inc(h_st[1], 16)
            sp.dma_start(prev_i, dst_prev).then_inc(prev_in, 16)
            sp.dma_start(dst_hi, dst_row.rearrange("t p -> (t p)").partition_broadcast(NR)).then_inc(row_in, 16)
            sp.wait_ge(rows_clear, 1)
            sp.dma_start(hbuf.rearrange("(a p) n -> p a n", p=P),
                         zero_row.unsqueeze(1).to_broadcast([P, NR, D])).then_inc(h_clear, 16)
            sp.wait_ge(table_ok, 1)
            sp.dma_start(ntab_d.rearrange("(a b) c -> a b c", b=P), ntab).then_inc(nt_st, 16)
            sp.wait_ge(table_ok, 2)
            sp.dma_start(ranks_d.rearrange("(a b) c -> a b c", b=P), ntab).then_inc(rk_st, 16)
            for k in range(2):
                sp.wait_ge(sc_st[k], NE // 2 * 16)
            sp.dma_start(em[0:ET, :, :], edges_d[0:NE * ET, :].rearrange("(t p) c -> p t c", p=ET)).then_inc(em_in, 16)
            sp.wait_ge(h_clear, 16)
            sp.wait_ge(setup_ok, 1)
            with sp.Fori(0, LAYERS) as L:
                pairs, its, pb, ib = layer_counts(sp, L)
                base = pb * 2
                for q in range(KB):
                    sp.wait_ge(w_ok, done(L * KB + q - 1))
                    sp.sem_inc(sp_tick, 1)
                    if q == 0:
                        sp.wait_ge(b_ok, done(L))
                        sp.sem_inc(sp_tick, 1)
                    sp.dma_start(w_raw[:, q % 2, :], Ws[bass.ds(L, 1), q * P:(q + 1) * P, :]
                                 .rearrange("a p n -> p (a n)")).then_inc(raw_in[q % 2], 16)
                sp.wait_ge(w_ok, done(L * KB + KB))
                sp.sem_inc(sp_tick, 1)
                sp.dma_start(b_raw[0:2, 0, :], bs[bass.ds(L, 1), :].rearrange("a n -> (a n)")
                             .partition_broadcast(2)).then_inc(b_in, 16)
                sp.wait_ge(u_ok, done(base))
                sp.sem_inc(sp_tick, 1)
                sp.wait_ge(agg_ok, done(ib * UN + its * UN))
                sp.sem_inc(sp_tick, 1)
                sp.dma_start(gam, ln_g[bass.ds(L, 1), :].rearrange("a n -> (a n)")
                             .partition_broadcast(P)).then_inc(gb_in, 16)
                sp.dma_start(bet[:, :], ln_b[bass.ds(L, 1), :].rearrange("a n -> (a n)")
                             .partition_broadcast(P)).then_inc(gb_in, 16)
                with sp.Fori(0, pairs) as pair:
                    c = pair * 2
                    for k in range(2):
                        j = base + c
                        sp.wait_ge(h_ok, done(j + k + 1))
                        sp.sem_inc(sp_tick, 1)
                        sp.dma_start(hbuf[bass.ds((c + k) * P, P), :], rows[:, 2 + k, :])\
                          .then_inc(h_st[k], 16)

            sp.wait_ge(lo_ok, done(all_tiles(sp)))
            sp.sem_inc(sp_tick, 1)

            def load(t, k, n):
                if not isinstance(t, int):
                    sp.wait_ge(f_o, done(t + k - FS + 1))
                    sp.sem_inc(sp_tick, 1)
                sp.dma_start(xs[0:n, k, :], x[bass.ds((t + k) * P, n), :]).then_inc(xf_in[k], 16)

            def store(t, k, n):
                sp.wait_ge(f_o, done(t + k + 1))
                sp.sem_inc(sp_tick, 1)
                sp.dma_start(out[bass.ds((t + k) * P, n), :], of[0:n, k, :])\
                  .then_inc(o_st[k] if n == P else o_last, 16)

            for k in range(FS):
                load(0, k, P)
            with sp.Fori(0, (FLOOP - FS) // FS) as group:
                t = group * FS
                for k in range(FS):
                    store(t, k, P)
                    load(t + FS, k, P)
            for k in range(FS):
                store(FLOOP - FS, k, P)
                if FLOOP + k < FULL:
                    sp.dma_start(xs[:, k, :], x[(FLOOP + k) * P:(FLOOP + k + 1) * P, :]).then_inc(xf_in[k], 16)
                elif FLOOP + k == FULL:
                    sp.dma_start(xs[0:TAIL, k, :], x[FULL * P:N, :]).then_inc(xf_in[k], 16)
            for k in range(FULL - FLOOP):
                store(FLOOP, k, P)
            store(FLOOP, FULL - FLOOP, TAIL)
            for k in range(FS):
                sp.wait_ge(o_st[k], 16 * (FLOOP // FS + (FLOOP + k < FULL)))
            sp.wait_ge(o_last, 16)

        @block.gpsimd
        def _(pool):
            g = nc.gpsimd
            for s in (rs_ok, var_ok, cp_idx, lo_ok):
                pool.sem_inc(s, PRIME)
            g.memset(zero_row, 0.0).then_inc(rows_clear, 1)
            g.iota(node_i, pattern=[[1, P]], base=0, channel_multiplier=P).then_inc(p_step, 1)
            g.iota(iota_i, pattern=[[1, P]], base=0, channel_multiplier=0).then_inc(p_step, 1)
            g.iota(rows_i, pattern=[[0, 1]], base=0, channel_multiplier=1).then_inc(p_step, 1)
            g.memset(mhalf[:, :], -0.5).then_inc(p_step, 1)
            g.memset(ones, 1.0).then_inc(p_step, 1)
            g.memset(before_p, 1.0).then_inc(p_step, 1)
            g.memset(ident, 0.0).then_inc(p_step, 1)
            g.memset(pick, 1.0).then_inc(p_step, 1)
            g.memset(negm[:, :], -1.0).then_inc(p_step, 1)
            pool.wait_ge(p_step, 9)
            g.affine_select(out=before_p, in_=before_p, compare_op=ALU.is_gt, fill=0.0, base=0,
                            pattern=[[1, P]], channel_multiplier=-1).then_inc(p_step, 1)
            g.affine_select(out=ident, in_=ident, compare_op=ALU.not_equal, fill=1.0, base=0,
                            pattern=[[-1, P]], channel_multiplier=1).then_inc(p_step, 1)
            g.affine_select(out=pick, in_=pick, compare_op=ALU.is_equal, fill=0.0, base=-(ET - 1),
                            pattern=[[0, P]], channel_multiplier=1).then_inc(p_step, 1)
            g.affine_select(out=negm[:, :], in_=negm[:, :], compare_op=ALU.not_equal, fill=0.0, base=0,
                            pattern=[[0, 1]], channel_multiplier=1).then_inc(p_step, 1)
            for first, table, stored_ok, ends in ((0, ntab_d, nt_st, dst_i), (NE, ranks_d, rk_st, src_i)):
                pool.wait_ge(stored_ok, 16)
                with pool.Fori(0, NE // TS) as group:
                    i = group * TS
                    for half in range(2):
                        own = slice(half * TS // 2, (half + 1) * TS // 2)
                        pool.wait_ge(tg_cp, done(first + i + (half - 1) * TS // 2))
                        pool.sem_inc(tick, 1)
                        g.tensor_copy(slot2[:, own], ends[:, bass.ds(i + half * TS // 2, TS // 2)]).then_inc(cp_idx, 1)
                        pool.wait_ge(cp_idx, done(first * 2 // TS + group * 2 + half + 1))
                        pool.sem_inc(tick, 1)
                        for k in range(own.start, own.stop):
                            g.indirect_dma_start(out=tslot[:, k, :], out_offset=None, in_=table[:, :],
                                                 in_offset=bass.IndirectOffsetOnAxis(ap=slot2[:, k:k + 1], axis=0))\
                             .then_inc(tg_in[k], 16)
            with pool.Fori(0, NE // (2 * ES)) as group:
                for half in range(2):
                    pool.wait_ge(pay_ok, group * 4 + half * 2 + 2)
                    pool.sem_inc(tick, 1)
                    for k in range(half * ES, half * ES + ES):
                        g.indirect_dma_start(out=edges_d[:, :],
                                             out_offset=bass.IndirectOffsetOnAxis(ap=slot2[0:ET, k:k + 1], axis=0),
                                             in_=pay_slot[0:ET, k, :], in_offset=None).then_inc(sc_st[half], 16)
            pool.wait_ge(setup_ok, 1)

            def sum_stage(L, table, its, ib):
                with pool.Fori(0, its) as group:
                    i = ib * UN + group * UN
                    for k in range(UN):
                        if k % GS == 0:
                            pool.wait_ge(ix_ok, ib * 2 + L + group * 2 + k // GS + 1)
                            pool.sem_inc(tick, 1)
                        pool.wait_ge(agg_ok, done(i + k - GS + 1))
                        pool.sem_inc(tick, 1)
                        g.indirect_dma_start(out=rows[:, k % GS, :], out_offset=None, in_=table[:, :],
                                             in_offset=bass.IndirectOffsetOnAxis(ap=slot[:, k:k + 1], axis=0))\
                         .then_inc(g_in[k % GS], 16)

            def low(j, c, k):
                pool.wait_ge(hi_ok, done(j + 1))
                pool.sem_inc(tick, 1)
                g.tensor_tensor(s_lo[:, k, :, :], agg_t[:, :, bass.ds(c * P, P)], s_hi[:, k, :, :].bitcast(f32),
                                ALU.subtract).then_inc(lo_ok, 1)

            def inverse(j, k):
                pool.wait_ge(mv_ok, done(j + 1))
                pool.sem_inc(tick, 1)
                g.tensor_scalar(var[:, k:k + 1], mv[:, k, 1:2], EPS, None, ALU.add).then_inc(var_ok, 1)
                pool.wait_ge(var_ok, done(j + 1))
                g.tensor_tensor(rstd[:, k:k + 1], var[:, k:k + 1], mhalf[:, :], ALU.pow).then_inc(rs_ok, 1)

            def w_stage(pairs, pb):
                base, nb = pb * 2, pairs * 2
                low(base, 0, 0)
                low(base + 1, 1, 1)
                with pool.Fori(0, pairs - 1) as pair:
                    c = pair * 2
                    for k in range(2):
                        low(base + c + k + 2, c + k + 2, k)
                        inverse(base + c + k, k)
                inverse(base + nb - 2, 0)
                inverse(base + nb - 1, 1)

            def stored(n):
                for k in range(2):
                    pool.wait_ge(h_st[k], 16 + n * 8)
                    pool.sem_inc(tick, 1)

            pairs, its, pb, ib = layer_counts(pool, 0)
            sum_stage(0, x, its, ib)
            w_stage(pairs, pb)
            with pool.Fori(1, LAYERS) as L:
                pairs, its, pb, ib = layer_counts(pool, L)
                stored(pb * 2)
                sum_stage(L, hbuf, its, ib)
                w_stage(pairs, pb)
            stored(all_tiles(pool))
            IDX1 = 2 * NE // (TS // 2)

            def indices(t, half):
                g.tensor_copy(slot2[:, half * FS:half * FS + FS], idx_f[:, bass.ds(t, FS)]).then_inc(cp_idx, 1)
                pool.wait_ge(cp_idx, done(IDX1 + t // FS + 1) if isinstance(t, int) else done(IDX1 + 1) + t // FS)
                pool.sem_inc(tick, 1)

            def gather(t, k, n, half):
                if not isinstance(t, int) or t > 0:
                    pool.wait_ge(f_sum, done(t + k - FS + 1))
                    pool.sem_inc(tick, 1)
                g.indirect_dma_start(out=hf[0:n, k, :], out_offset=None, in_=hbuf[:, :],
                                     in_offset=bass.IndirectOffsetOnAxis(
                                         ap=slot2[0:n, half * FS + k:half * FS + k + 1], axis=0))\
                 .then_inc(hf_in[k], 16)

            def rstd_of(t, k, n):
                pool.wait_ge(f_ve, done(t + k + 1))
                g.tensor_tensor(rstd[0:n, k:k + 1], var[0:n, k:k + 1], mhalf[0:n, :], ALU.pow).then_inc(f_rs, 1)

            pool.sem_inc(f_rs, PRIME)
            indices(0, 0)
            for k in range(FS):
                gather(0, k, P, 0)

            def group_of(t, half):
                indices(t + FS, half)
                for k in range(FS):
                    gather(t + FS, k, P, half)
                    rstd_of(t, k, P)

            LATER = FLOOP // FS - 2
            group_of(0, 1)
            with pool.Fori(0, LATER // 2) as group:
                for half in range(2):
                    group_of((group * 2 + half + 1) * FS, half)
            assert LATER % 2 == 1
            group_of(LATER * FS, 0)
            indices(FLOOP, 1)
            for k in range(FS):
                if FLOOP + k <= FULL:
                    gather(FLOOP, k, P if FLOOP + k < FULL else TAIL, 1)
                rstd_of(FLOOP - FS, k, P)
            for k in range(FULL - FLOOP + 1):
                rstd_of(FLOOP, k, P if FLOOP + k < FULL else TAIL)

        @block.vector
        def _(dve):
            v = nc.vector
            for s in (w_ok, b_ok, mv_ok, t_ok, u_ok, edge_ok, st_ok, f_sum, f_st, f_mv, f_o):
                dve.sem_inc(s, PRIME)
            steps = [0]

            def link(ins, *also):
                steps[0] += 1
                ins.then_inc(v_step, 1)
                dve.wait_ge(v_step, steps[0])

            link(v.memset(zero_bf, 0.0))
            link(v.memset(ones2[:, :].bitcast(f32), 1.0))
            link(v.memset(ntab, 0.0))
            link(v.memset(q0b, 0.0))
            link(v.memset(zcol[:, :], 0.0))
            dve.wait_ge(h_st[0], 16)
            dve.wait_ge(h_st[1], 16)
            for n, e in enumerate((src_i, dst_i)):
                link(v.tensor_scalar(hilo_i[:, 2 * n, :], e, 7, None, ALU.logical_shift_right))
                link(v.tensor_scalar(hilo_i[:, 2 * n + 1, :], e, P - 1, None, ALU.bitwise_and))
            link(v.tensor_copy(hilo, hilo_i))
            link(v.memset(idx_now[:, NE:], 0.0))
            link(v.memset(idx_h[:, NE:], 0.0))
            link(v.memset(em, 0.0))
            link(v.memset(all_ones, 1.0))
            link(v.tensor_scalar(pay[:, :, 3], src_i, float(N - 1), None, ALU.min))
            dve.wait_ge(p_step, 13)
            link(v.tensor_copy(iota[:, :], iota_i))
            link(v.tensor_copy(iota_b, iota_i))
            for n, h in enumerate(hot):
                w = h.shape[2]
                v.tensor_tensor(h, iota_b[:, 0:w].unsqueeze(1).to_broadcast([P, NE, w]),
                                hilo[:, n, :].unsqueeze(2).to_broadcast([P, NE, w]), ALU.is_equal)\
                 .then_inc(hot_ok, 1)
            dve.wait_ge(row_in, 16)
            link(v.tensor_copy(row_no, rows_i))
            link(v.tensor_scalar(dst_hi, dst_hi, 7, None, ALU.logical_shift_right))
            link(v.tensor_scalar(at_hi, dst_hi, row_no, None, ALU.is_equal))
            link(v.tensor_scalar(valid, node_i, float(N), None, ALU.is_lt))
            dve.wait_ge(hist_ok, 2)
            link(v.tensor_copy(outs, ps_s[0][0:NR, 0:P]))
            link(v.tensor_copy(ins, ps_y[0][0:NR, 0:P]))
            v.tensor_scalar(t1, outs, 1.0, None, ALU.max).then_inc(deg_ok, 1)
            v.tensor_scalar(t2, ins, 1.0, None, ALU.max).then_inc(deg_ok, 1)
            link(v.scalar_tensor_tensor(sets[:, 0, :], ins, 0.0, valid, ALU.is_gt, ALU.mult))
            link(v.scalar_tensor_tensor(only[:, 0, :], outs, 0.0, valid, ALU.is_gt, ALU.mult))
            link(v.tensor_tensor(sets[:, 1, :], only[:, 0, :], sets[:, 0, :], ALU.mult))
            v.tensor_copy(flags_b, only[:, 0, :]).then_inc(flags_ok, 1)
            dve.wait_ge(pow_ok, 2)
            for deg, root in ((t1, r1), (t2, r2)):
                link(v.reciprocal(root, root))
                link(v.tensor_tensor(deg, deg, root, ALU.mult))
                link(v.tensor_tensor(deg, deg, root, ALU.mult))
                link(v.tensor_scalar(deg, deg, -0.5, 1.5, ALU.mult, ALU.add))
            link(v.tensor_tensor(ntab[:, :, C_NOUT], t1, r1, ALU.mult))
            link(v.tensor_tensor(t2, t2, r2, ALU.mult))
            link(v.tensor_tensor(ntab[:, :, C_NIN], t2, valid, ALU.mult))
            v.engine_nop().then_inc(table_ok, 1)
            CH = NE // 4
            dve.wait_ge(prev_in, 16)
            link(v.tensor_tensor(is_new, dst_i, prev_i, ALU.not_equal))
            link(v.tensor_scalar(sets_of, dst_i, float(N), None, ALU.is_lt))

            def flags_of(lev, c):
                for n in range(c * CH // 4, (c + 1) * CH // 4):
                    dve.wait_ge(gath_ok, lev * CH + n + 1)
                    v.tensor_tensor(picked[:, n * 4:n * 4 + 4, :], ps_a[n % 4][:, :, :],
                                    hot[3][:, n * 4:n * 4 + 4, :], ALU.mult).then_inc(pick_f, 1)
                own = slice(c * CH, c * CH + CH)
                dve.wait_ge(pick_f, lev * CH + (c + 1) * CH // 4)
                link(v.tensor_reduce(flag_e[:, own], picked[:, own, :], mybir.AxisListType.X, ALU.add))
                return own

            for lev in range(LEVELS):
                for c in range(4):
                    own = flags_of(lev, c)
                    v.tensor_tensor(hot_f[:, own, :], hot[0][:, own, :],
                                    flag_e[:, own].unsqueeze(2).to_broadcast([P, CH, NR]), ALU.mult)\
                     .then_inc(fl_ok, 1)
                link(v.tensor_tensor(sets_of, sets_of, flag_e, ALU.add))
                dve.wait_ge(lev_ok, lev + 1)
                link(v.scalar_tensor_tensor(only[:, 0, :], ps_y[1][0:NR, 0:P], 0.0, valid, ALU.is_gt, ALU.mult))
                link(v.tensor_tensor(sets[:, lev + 2, :], only[:, 0, :], sets[:, 0, :], ALU.mult))
                if lev < LEVELS - 1:
                    v.tensor_copy(flags_b, only[:, 0, :]).then_inc(flags_ok, 1)
                else:
                    link(v.tensor_copy(flags_b, only[:, 0, :]))
            link(v.tensor_copy(only[:, SETS - 1, :], sets[:, SETS - 1, :]))
            link(v.tensor_tensor(only[:, 0:SETS - 1, :], sets[:, 0:SETS - 1, :], sets[:, 1:SETS, :], ALU.subtract))
            for n in range(SETS):
                link(v.tensor_tensor_scan(scans[:, n, :], ones_np, only[:, n, :], 0.0, ALU.mult, ALU.add))
            for n in range(SETS):
                v.tensor_copy(row_sums[:, n:n + 1], scans[:, SETS - 1 - n, P - 1:P]).then_inc(sums_ok, 1)
            dve.wait_ge(pre_ok, 2)
            link(v.tensor_copy(before, ps_s[0][0:NR, 0:SETS]))
            link(v.tensor_copy(totals, ps_s[1][:, 0:SETS]))
            link(v.tensor_tensor_scan(reach, ones[:, 0:SETS], totals, 0.0, ALU.mult, ALU.add))
            link(v.tensor_tensor(before, before, reach[0:NR, :], ALU.add))
            link(v.tensor_tensor(before, before, totals[0:NR, :], ALU.subtract))
            for n in range(SETS):
                link(v.scalar_tensor_tensor(scans[:, n, :], scans[:, n, :], before[:, SETS - 1 - n:SETS - n],
                                            only[:, n, :], ALU.add, ALU.mult))
            for n in range(1, SETS):
                link(v.tensor_tensor(scans[:, 0, :], scans[:, 0, :], scans[:, n, :], ALU.add))
            dve.wait_ge(nt_st, 16)
            link(v.tensor_copy(ntab[:, :, C_ROW], scans[:, 0, :]))
            v.engine_nop().then_inc(table_ok, 1)
            v.tensor_copy(fidx, scans[:, 0, :]).then_inc(fid_ok, 1)
            dve.wait_ge(fidt_ok, 1)
            link(v.tensor_copy(idx_f[:, :], ps_s[0][:, 0:NR]))
            v.engine_nop().then_inc(flags_ok, 1)
            for pad in (wgt, rel):
                link(v.memset(pad[:, NE:NE + 2], 0.0))
            for c in range(4):
                flags_of(LEVELS, c)
            link(v.tensor_tensor(sets_of, sets_of, flag_e, ALU.add))
            for n in range(SETS + 1):
                link(v.tensor_scalar(keep[:, n, :], sets_of, float(SETS - n), None, ALU.is_equal))
            link(v.tensor_tensor(fresh, keep, is_new.unsqueeze(1).to_broadcast([P, SETS + 1, NE]), ALU.mult))
            v.engine_nop().then_inc(keep_ok, 1)
            dve.wait_ge(place_ok, 4)

            def before_in_set(out, in_tile, in_tiles):
                flat = "p a b -> p (a b)"
                link(v.tensor_copy(col_sum.rearrange(flat), in_tiles))
                link(v.tensor_tensor_scan(col_scan.rearrange(flat), all_ones, col_sum.rearrange(flat), 0.0,
                                          ALU.mult, ALU.add))
                link(v.tensor_tensor(pos, col_scan, col_sum, ALU.subtract))
                link(v.tensor_tensor(pos.rearrange(flat), in_tile, pos.rearrange(flat), ALU.add))
                link(v.tensor_tensor(pos, pos, keep, ALU.mult))
                link(v.tensor_tensor(out, pos[:, 0, :], pos[:, 1, :], ALU.add))
                for n in range(2, SETS + 1):
                    link(v.tensor_tensor(out, out, pos[:, n, :], ALU.add))

            cols = (SETS + 1) * NE
            before_in_set(place, ps_y[0][:, 0:cols], ps_y[1][:, 0:cols])
            link(v.tensor_tensor(place, place, is_new, ALU.add))
            link(v.tensor_scalar(past, keep[:, SETS, :], -1.0, 1.0, ALU.mult, ALU.add))
            link(v.tensor_tensor(place, place, past, ALU.mult))
            link(v.tensor_scalar(past, keep[:, SETS, :], reach[:, SETS - 1:SETS], None, ALU.mult))
            link(v.tensor_tensor(past, past, keep[:, SETS, :], ALU.add))
            link(v.tensor_tensor(pay[:, :, 2], place, past, ALU.add))
            before_in_set(place, ps_s[2][:, 0:cols], ps_s[3][:, 0:cols])
            link(v.tensor_copy(target, place))
            link(v.tensor_scalar(cnt_f, reach[0:1, :], float(2 * P), None, ALU.add))
            link(v.tensor_copy(cnt_i, cnt_f))
            link(v.tensor_scalar(cnt_i, cnt_i, 8, None, ALU.logical_shift_right))
            link(v.tensor_scalar(cnt_f, cnt_i, float(PAIRS_MIN), None, ALU.max))
            link(v.tensor_copy(ends, col_scan[0:1, 0:SETS, NE - 1]))
            for n in range(SETS):
                link(v.tensor_scalar(limits[:, n, :], iota[0:1, 0:NE // UN], float(UN * ET), ends[:, n:n + 1],
                                     ALU.mult, ALU.is_lt))
            link(v.tensor_reduce(its_f, limits, mybir.AxisListType.X, ALU.add))
            link(v.tensor_scalar(its_f, its_f, float(ITS_MIN), None, ALU.max))
            for n, (f, least, own, base) in enumerate(((cnt_f, PAIRS_MIN, pairs_t, base_p),
                                                       (its_f, ITS_MIN, its_t, base_i))):
                for L in range(LAYERS):
                    c = max(0, L - (LAYERS - SETS))
                    link(v.tensor_copy(lay_f[:, n, L:L + 1], f[:, c:c + 1]))
                link(v.tensor_tensor_scan(lay_f[:, 2 + n, :], ones[0:1, 0:LAYERS], lay_f[:, n, :], 0.0,
                                          ALU.mult, ALU.add))
                link(v.tensor_tensor(base[:, :], lay_f[:, 2 + n, :], lay_f[:, n, :], ALU.subtract))
                link(v.tensor_scalar(own[:, :], lay_f[:, n, :], float(-least), None, ALU.add))

            dve.wait_ge(tg_cp, done(2 * NE))
            link(v.tensor_tensor(pay[:, :, 1], dtab[:, :, C_NIN], stab[:, :, C_NOUT], ALU.mult))
            link(v.tensor_copy(pay[:, :, 0], stab[:, :, C_ROW]))

            def edges_out(i, half):
                own = slice(half * ES, half * ES + ES)
                v.tensor_copy(slot2[:, own], target[:, bass.ds(i + half * ES, ES)]).then_inc(pay_ok, 1)
                v.tensor_copy(pay_slot[:, own, :], pay[:, bass.ds(i + half * ES, ES), :]).then_inc(pay_ok, 1)

            for half in range(2):
                edges_out(0, half)
            with dve.Fori(1, NE // (2 * ES)) as group:
                for half in range(2):
                    dve.wait_ge(sc_st[half], group * (ES * 16))
                    dve.sem_inc(dve_tick, 1)
                    edges_out(group * (2 * ES), half)
            dve.wait_ge(em_in, 16)
            v.engine_nop().then_inc(keep_ok, 1)
            link(v.tensor_copy(wgt[:, 0:NE], em[:, :, 1]))
            link(v.tensor_copy(idx_h[:, 0:NE], em[:, :, 0]))
            link(v.tensor_copy(idx_now[:, 0:NE], em[:, :, 3]))
            dve.wait_ge(pick_ok, 1)
            link(v.tensor_copy(q0b[:, 1:NE], ps_s[0][:, 0:NE - 1]))
            link(v.tensor_tensor(rel[:, 0:NE], em[:, :, 2], q0b, ALU.subtract))
            link(v.tensor_copy(q0[:, :], q0b[0:1, :]))
            v.engine_nop().then_inc(setup_ok, 1)

            def select(i, k):
                v.tensor_scalar(sel[:, k % 2, :], iota[:, :], rel[:, bass.ds(i, 1)], wgt[:, bass.ds(i, 1)],
                                ALU.is_equal, ALU.mult).then_inc(sel_ok, 1)

            def indices(t, half):
                v.tensor_copy(slot[:, half * GS:half * GS + GS], idx_now[:, bass.ds(t, GS)]).then_inc(ix_ok, 1)

            def zero_tail(nb):
                v.tensor_copy(agg_t[:, :, bass.ds((nb - 2) * P, 2 * P)],
                              zcol[:, :].unsqueeze(2).to_broadcast([P, KB, 2 * P])).then_inc(v_tail, 1)

            def sum_stage(L, its, pb, ib, nb):
                base = pb * 2
                dve.wait_ge(lo_ok, done(base))
                dve.sem_inc(dve_tick, 1)
                zero_tail(nb)
                v.memset(agg_t[:, :, 0:1], 0.0).then_inc(zero_ok, 1)
                indices(0, 0)
                for k in range(2):
                    select(k, k)
                def tiles(first, end):
                    with dve.Fori(first, end) as group:
                        t = group * UN
                        i = ib * UN + t
                        for k in range(UN):
                            r0 = dve.value_load(q0[0:1, bass.ds(t + k, 1)], min_val=0, max_val=N + 1)
                            dve.wait_ge(agg_ok, done(i + k + 1))
                            select(t + k + 2, k)
                            dve.wait_ge(edge_ok, done(i + k))
                            dve.sem_inc(dve_tick, 1)
                            dve.wait_ge(ev_ok, done(i + k + 1))
                            col = agg_t[:, :, bass.ds(r0, 1)]
                            v.tensor_tensor(col, ps_a[k % GS][:, :, 0:1], col, ALU.add).then_inc(edge_ok, 1)
                            if k % GS == 0:
                                indices(t + k + GS, 1 - k // GS)

                for q in range(KB):
                    if q % 2 == 0:
                        tiles(q // 2, q // 2 + 1)
                    if q == 0:
                        dve.wait_ge(y_ok, done(base))
                        dve.sem_inc(dve_tick, 1)
                    dve.wait_ge(raw_in[q % 2], (L * 2 + q // 2 + 1) * 16)
                    dve.sem_inc(dve_tick, 1)
                    v.tensor_copy(w_hi[:, q, :], w_raw[:, q % 2, :]).then_inc(wh_ok, 1)
                    dve.wait_ge(wh_ok, L * KB + q + 1)
                    v.tensor_tensor(w_lo[:, q, :], w_raw[:, q % 2, :], w_hi[:, q, :].bitcast(f32), ALU.subtract)\
                     .then_inc(w_ok, 1)
                dve.wait_ge(b_in, (L + 1) * 16)
                dve.sem_inc(dve_tick, 1)
                v.tensor_copy(b_high, b_raw[0:2, 0, :]).then_inc(bh_ok, 1)
                dve.wait_ge(bh_ok, L + 1)
                v.scalar_tensor_tensor(b_rows[:, :], b_high.bitcast(f32), negm[:, :], b_raw[0:2, 0, :],
                                       ALU.mult, ALU.add).then_inc(b_ok, 1)
                tiles(2, its)
                v.tensor_copy(idx_now[:, :], idx_h[:, :]).then_inc(now_ok, 1)

            def centre(j, k):
                dve.wait_ge(y_ok, done(j + 1))
                v.bn_stats(stats[:, k, :], ps_y[k][:, :]).then_inc(st_ok, 1)
                dve.wait_ge(st_ok, done(j + 1))
                dve.sem_inc(dve_tick, 1)
                v.bn_aggr(mv[:, k, :], stats[:, k, :]).then_inc(mv_ok, 1)
                dve.wait_ge(h_ok, done(j - 1))
                dve.wait_ge(mv_ok, done(j + 1))
                dve.sem_inc(dve_tick, 1)
                v.scalar_tensor_tensor(rows[:, k, :], ps_y[k][:, :], mv[:, k, 0:1], gam,
                                       ALU.subtract, ALU.mult).then_inc(t_ok, 1)

            def scale(j, k):
                dve.wait_ge(t_ok, done(j + 1))
                dve.sem_inc(dve_tick, 1)
                dve.wait_ge(rs_ok, done(j + 1))
                v.scalar_tensor_tensor(rows[:, k, :], rows[:, k, :], rstd[:, k:k + 1], bet[:, :],
                                       ALU.mult, ALU.add).then_inc(u_ok, 1)

            def w_stage(L, pairs, pb):
                base, nb = pb * 2, pairs * 2
                dve.wait_ge(gb_in, (L + 1) * 32)
                dve.sem_inc(dve_tick, 1)
                centre(base, 0)
                with dve.Fori(0, pairs - 1) as pair:
                    j = base + pair * 2
                    for k in range(2):
                        centre(j + k + 1, 1 - k)
                        scale(j + k, k)
                centre(base + nb - 1, 1)
                scale(base + nb - 2, 0)
                scale(base + nb - 1, 1)

            link(v.memset(agg_t[:, :, 1:4 * P], 0.0))
            with dve.Fori(0, LAYERS) as L:
                pairs, its, pb, ib = layer_counts(dve, L)
                sum_stage(L, its, pb, ib, pairs * 2)
                w_stage(L, pairs, pb)

            def width(n):
                return P if n < FULL else TAIL

            def step(t, k, first=False):
                end = isinstance(t, int)
                if not end or t + k + 2 <= FULL:
                    t2, k2 = t + (k + 2) // FS * FS, (k + 2) % FS
                    n2 = width(t + k + 2) if end else P
                    add(t2, k2, n2)
                if not end or t + k + 1 <= FULL:
                    mean(t + (k + 1) // FS * FS, (k + 1) % FS, width(t + k + 1) if end else P)
                if not end or t + k + 2 <= FULL:
                    spread(t2, k2, n2)
                result(t, k, width(t + k) if end else P, first)

            def add(t, k, n):
                for arrived in (xf_in, hf_in):
                    dve.wait_ge(arrived[k], t * (16 // FS) + 16)
                    dve.sem_inc(dve_tick, 1)
                v.tensor_tensor(xs[0:n, k, :], xs[0:n, k, :], hf[0:n, k, :], ALU.add).then_inc(f_sum, 1)

            def spread(t, k, n):
                dve.wait_ge(f_sum, done(t + k + 1))
                v.bn_stats(stats[0:n, k, :], xs[0:n, k, :]).then_inc(f_st, 1)

            def mean(t, k, n):
                dve.wait_ge(f_st, done(t + k + 1))
                dve.sem_inc(dve_tick, 1)
                v.bn_aggr(mv[0:n, k, :], stats[0:n, k, :]).then_inc(f_mv, 1)

            def result(t, k, n, first):
                dve.wait_ge(f_mv, done(t + k + 1))
                dve.sem_inc(dve_tick, 1)
                dve.wait_ge(f_rs, done(t + k + 1))
                dve.sem_inc(dve_tick, 1)
                if not first:
                    dve.wait_ge(o_st[k], t * (16 // FS))
                    dve.sem_inc(dve_tick, 1)
                v.tensor_scalar(of[0:n, k, :], xs[0:n, k, :], mv[0:n, k, 0:1], rstd[0:n, k:k + 1],
                                ALU.subtract, ALU.mult).then_inc(f_o, 1)

            for k in range(2):
                add(0, k, P)
                spread(0, k, P)
            mean(0, 0, P)
            for k in range(FS):
                step(0, k, first=True)
            with dve.Fori(1, FLOOP // FS - 1) as group:
                for k in range(FS):
                    step(group * FS, k)
            for n in range(FLOOP - FS, FULL + 1):
                step(n - n % FS, n % FS)

        @block.scalar
        def _(act):
            a = nc.scalar
            for s in (tg_cp, ev_ok, hi_ok, h_ok):
                act.sem_inc(s, PRIME)
            act.wait_ge(deg_ok, 2)
            a.activation(r1, t1, ACT.Sqrt).then_inc(pow_ok, 1)
            a.activation(r2, t2, ACT.Sqrt).then_inc(pow_ok, 1)
            act.preload_act_table(ACT.Gelu)
            def hold(s, n):
                act.wait_ge(s, n)
                act.sem_inc(act_tick, 1)

            for first, table in ((0, dtab), (NE, stab)):
                with act.Fori(0, NE // TS) as group:
                    i = group * TS
                    for k in range(TS):
                        hold(tg_in[k], (first // TS) * 16 + group * 16 + 16)
                        a.activation(table[:, bass.ds(i + k, 1), :], tslot[:, k:k + 1, :], ACT.Copy).then_inc(tg_cp, 1)
            act.wait_ge(setup_ok, 1)

            def sum_stage(its, pb, ib):
                hold(lo_ok, done(pb * 2))
                with act.Fori(0, its) as group:
                    t = group * UN
                    for k in range(UN):
                        i = ib * UN + t
                        r0 = act.value_load(q0[0:1, bass.ds(t + k, 1)], min_val=0, max_val=N + 1)
                        hold(agg_ok, done(i + k + 1))
                        hold(ev_ok, done(i + k))
                        a.activation(agg_t[:, :, bass.ds(r0 + 1, P - 1)], ps_a[k % GS][:, :, 1:P], ACT.Copy)\
                         .then_inc(ev_ok, 1)

            def high(j, c, k):
                hold(y_ok, done(j - 1))
                a.activation(s_hi[:, k, :, :], agg_t[:, :, bass.ds(c * P, P)], ACT.Copy).then_inc(hi_ok, 1)

            def gelu(j, j_pair, k):
                hold(u_ok, done(j + 1))
                hold(h_st[k], j_pair * 8 + 16)
                a.activation(rows[:, 2 + k, :], rows[:, k, :], ACT.Gelu).then_inc(h_ok, 1)

            def w_stage(L, pairs, its, pb, ib):
                base, nb = pb * 2, pairs * 2
                hold(edge_ok, done(ib * UN + its * UN))
                hold(ev_ok, done(ib * UN + its * UN))
                hold(b_ok, done(L + 1))
                for n in range(3):
                    high(base + n, n, n % 2)
                with act.Fori(0, pairs - 2) as pair:
                    c = pair * 2
                    for k in range(2):
                        j = base + c
                        high(j + k + 3, c + k + 3, 1 - k)
                        gelu(j + k, j, k)
                high(base + nb - 1, nb - 1, 1)
                for n in range(4, 0, -1):
                    gelu(base + nb - n, base + nb - n - n % 2, n % 2)

            with act.Fori(0, LAYERS) as L:
                pairs, its, pb, ib = layer_counts(act, L)
                sum_stage(its, pb, ib)
                w_stage(L, pairs, its, pb, ib)

            act.sem_inc(f_ve, PRIME)

            def add_eps(t, k, n):
                hold(f_mv, done(t + k + 1))
                a.activation(var[0:n, k:k + 1], mv[0:n, k, 1:2], ACT.Copy, bias=EPS).then_inc(f_ve, 1)

            with act.Fori(0, FLOOP // FS) as group:
                for k in range(FS):
                    add_eps(group * FS, k, P)
            for k in range(FULL - FLOOP + 1):
                add_eps(FLOOP, k, P if FLOOP + k < FULL else TAIL)

        @block.tensor
        def _(pe):
            mm = nc.tensor.matmul
            for s in (agg_ok, y_ok):
                pe.sem_inc(s, PRIME)
            def histogram(acc, high, low, chunk_ready=None):
                mm(acc, zero_bf[:, 0:NR], zero_bf, start=True, stop=False)
                for i in range(NE):
                    if chunk_ready is not None and i % (NE // 4) == 0:
                        pe.wait_ge(fl_ok, chunk_ready + i // (NE // 4) + 1)
                    m = mm(acc, high[:, i, :], low[:, i, :], start=False, stop=i == NE - 1)
                return m

            for n, acc in enumerate((ps_s[0][0:NR, 0:P], ps_y[0][0:NR, 0:P])):
                pe.wait_ge(hot_ok, 2 * n + 2)
                histogram(acc, hot[2 * n], hot[2 * n + 1]).then_inc(hist_ok, 1)
            def flags_of_rows(lev):
                pe.wait_ge(flags_ok, lev + 1)
                for n in range(NE // 4):
                    if lev * NE // 4 + n >= 4:
                        pe.wait_ge(pick_f, lev * NE // 4 + n - 3)
                    for b in range(4):
                        i = n * 4 + b
                        m = mm(ps_a[n % 4][:, b, :], at_hi[:, i * P:(i + 1) * P], flags_b, start=True, stop=True)
                    m.then_inc(gath_ok, 1)

            for lev in range(LEVELS):
                flags_of_rows(lev)
                histogram(ps_y[1][0:NR, 0:P], hot_f, hot[1], lev * 4).then_inc(lev_ok, 1)
            pe.wait_ge(sums_ok, SETS)
            mm(ps_s[0][0:NR, 0:SETS], lower, row_sums, start=True, stop=True).then_inc(pre_ok, 1)
            mm(ps_s[1][:, 0:SETS], ones_np, row_sums, start=True, stop=True).then_inc(pre_ok, 1)
            pe.wait_ge(fid_ok, 1)
            nc.tensor.transpose(ps_s[0][:, 0:NR], fidx, ident[0:NR, 0:NR]).then_inc(fidt_ok, 1)
            flags_of_rows(LEVELS)
            pe.wait_ge(keep_ok, 1)
            cols = (SETS + 1) * NE
            for marks, in_tile, in_tiles in ((fresh, ps_y[0], ps_y[1]), (keep, ps_s[2], ps_s[3])):
                marks = marks.rearrange("p a b -> p (a b)")
                mm(in_tile[:, 0:cols], before_p, marks, start=True, stop=True).then_inc(place_ok, 1)
                mm(in_tiles[:, 0:cols], ones[0:ET, :], marks[0:ET, :], start=True, stop=True).then_inc(place_ok, 1)
            pe.wait_ge(keep_ok, 2)
            mm(ps_s[0][:, 0:NE], pick, em[:, :, 2], start=True, stop=True).then_inc(pick_ok, 1)
            pe.wait_ge(setup_ok, 1)

            def sum_stage(L, its, ib):
                with pe.Fori(0, its) as group:
                    for k in range(UN):
                        i = ib * UN + group * UN
                        pe.wait_ge(g_in[k % GS], (ib * 2 + group * 2 + k // GS + 1) * 16)
                        pe.sem_inc(pe_tick, 1)
                        pe.wait_ge(sel_ok, i + L * 2 + k + 1)
                        pe.sem_inc(pe_tick, 1)
                        pe.wait_ge(ev_ok, done(i + k - GS + 1))
                        pe.wait_ge(edge_ok, done(i + k - GS + 1))
                        pe.sem_inc(pe_tick, 1)
                        for b in range(KB):
                            m = mm(ps_a[k % GS][:, b, :], rows[:, k % GS, b * P:(b + 1) * P], sel[:, k % 2, :],
                                   start=True, stop=True)
                        m.then_inc(agg_ok, 1)

            def w_stage(L, pairs, pb):
                base = pb * 2
                pe.wait_ge(w_ok, done(L * KB + KB))
                pe.sem_inc(pe_tick, 1)
                pe.wait_ge(b_ok, done(L + 1))
                pe.sem_inc(pe_tick, 1)
                with pe.Fori(0, pairs) as pair:
                    c = pair * 2
                    for k in range(2):
                        j = base + c
                        pe.wait_ge(t_ok, done(j + k - 1))
                        pe.sem_inc(pe_tick, 1)
                        mm(ps_y[k][:, :], ones2[:, :], b_rows[:, :], start=True, stop=False)
                        pe.wait_ge(hi_ok, done(j + k + 1))
                        pe.sem_inc(pe_tick, 1)
                        for b in range(KB):
                            mm(ps_y[k][:, :], s_hi[:, k, b, :], w_hi[:, b, :], start=False, stop=False)
                            mm(ps_y[k][:, :], s_hi[:, k, b, :], w_lo[:, b, :], start=False, stop=False)
                        pe.wait_ge(lo_ok, done(j + k + 1))
                        pe.sem_inc(pe_tick, 1)
                        for b in range(KB):
                            m = mm(ps_y[k][:, :], s_lo[:, k, b, :], w_hi[:, b, :], start=False, stop=b == KB - 1)
                        m.then_inc(y_ok, 1)

            with pe.Fori(0, LAYERS) as L:
                pairs, its, pb, ib = layer_counts(pe, L)
                sum_stage(L, its, ib)
                w_stage(L, pairs, pb)


def kernel(x, src, dst, L0_gnn_Ws, L0_gnn_bs, L0_gnn_ln_g, L0_gnn_ln_b):
    import numpy as np
    import concourse.bacc as bacc
    from concourse.bass_utils import run_bass_kernel_spmd as run

    def tiles(e):
        flat = np.full(NE * ET, N, e.dtype)
        flat[:E] = e
        laid = np.full((P, NE), N, e.dtype)
        laid[:ET] = flat.reshape(NE, ET).T
        return laid

    arrays = {"in_x": np.ascontiguousarray(x), "in_src": tiles(np.asarray(src)), "in_dst": tiles(np.asarray(dst)),
              "in_dst_prev": tiles(np.roll(np.append(np.asarray(dst), np.asarray(dst).dtype.type(N)), 1)[:E]),
              "in_dst_row": np.ascontiguousarray(tiles(np.asarray(dst)).T),
              "in_Ws": np.ascontiguousarray(L0_gnn_Ws), "in_bs": np.ascontiguousarray(L0_gnn_bs),
              "in_ln_g": np.ascontiguousarray(L0_gnn_ln_g), "in_ln_b": np.ascontiguousarray(L0_gnn_ln_b)}
    nc = bacc.Bacc("TRN2", target_bir_lowering=False, num_devices=1)
    args = [nc.dram_tensor(k, v.shape, mybir.dt.from_np(v.dtype), kind="ExternalInput").ap()
            for k, v in arrays.items()]
    args.append(nc.dram_tensor("out_0", (N, D), f32, kind="ExternalOutput").ap())
    build(nc, *args)
    return run(nc, [arrays], core_ids=[0]).results[0]["out_0"]
```
